# Optimizing a Trainium2 kernel written in Bass

```python
import numpy as np
import jax
import jax.numpy as jnp

def _softmax(x, axis=-1):
    return jax.nn.softmax(x, axis=axis)

def _gelu(x):
    return jax.nn.gelu(x, approximate=True)

def _silu(x):
    return jax.nn.silu(x)

def _sigmoid(x):
    return jax.nn.sigmoid(x)

def _layernorm(x, axis=-1, eps=1e-05):
    m = jnp.mean(x, axis=axis, keepdims=True)
    v = jnp.var(x, axis=axis, keepdims=True)
    return (x - m) / jnp.sqrt(v + eps)

def _scatter_add(tgt, idx, src, axis=0):
    return tgt.at[idx].add(src)

def _segment_sum(src, seg, n):
    return jax.ops.segment_sum(src, seg, n)
kernel_name = 'mk_adaln_d1_jaxref_r8_f227fe'

def setup_inputs(seed: int=0):
    np.random.seed(seed)
    _w = jnp.asarray

    def _L0_attn_setup():
        import jax, jax.numpy as jnp
        import numpy as np
        C = 128
        H = 8
        MAX_SAMPLES = 32
        HALF_S = MAX_SAMPLES // 2
        S = 2 * HALF_S
        K = 64
        MAX_FREQ = 16.0
        MIN_FREQ = 1.0
        MAX_RECEPTIVE = HALF_S * MAX_FREQ
        B, L = (2, 128)

        def _gather_conv(x, wave_w, wave_b, kernel_w, kernel_b, out_w):
            Bx, Lx, Cx = x.shape
            D = Cx // H
            wave = (x @ wave_w.T + wave_b).reshape(Bx, Lx, H, 2)
            freq = MIN_FREQ + jax.nn.sigmoid(wave[..., 0]) * (MAX_FREQ - MIN_FREQ)
            phase = jnp.tanh(wave[..., 1]) * freq
            taps = jnp.arange(S, dtype=x.dtype) - HALF_S + 0.5
            offs = phase[..., None] + freq[..., None] * taps
            pos = jnp.arange(Lx, dtype=x.dtype)[None, :, None, None] + offs
            pos = jnp.clip(pos, 0.0, Lx - 1)
            i0f = jnp.floor(pos)
            frac = pos - i0f
            i0 = i0f.astype(jnp.int32)
            i1 = jnp.minimum(i0 + 1, Lx - 1)
            xh = x.reshape(Bx, Lx, H, D)
            b_idx = jnp.arange(Bx)[:, None, None, None]
            h_idx = jnp.arange(H)[None, None, :, None]
            g0 = xh[b_idx, i0, h_idx]
            g1 = xh[b_idx, i1, h_idx]
            gathered = g0 + frac[..., None] * (g1 - g0)
            kmat = (x @ kernel_w.T + kernel_b).reshape(Bx, Lx, H, K)
            bins = jnp.clip(jnp.floor((offs + MAX_RECEPTIVE) / (2.0 * MAX_RECEPTIVE) * K).astype(jnp.int32), 0, K - 1)
            w = jnp.take_along_axis(kmat, bins, axis=3)
            y = jnp.einsum('blhs,blhsd->blhd', w, gathered).reshape(Bx, Lx, Cx)
            return y @ out_w.T
        key = jax.random.key(seed)
        k1, k2, k3, k4 = jax.random.split(key, 4)
        x = jax.random.normal(k1, (B, L, C), dtype=jnp.float32)
        wave_w = 0.02 * jax.random.normal(k2, (2 * H, C), dtype=jnp.float32)
        wave_b = jnp.zeros((2 * H,), dtype=jnp.float32)
        lim_k = 0.1 * np.sqrt(6.0 / (H * K + C))
        kernel_w = jax.random.uniform(k3, (H * K, C), dtype=jnp.float32, minval=-lim_k, maxval=lim_k)
        kernel_b = jnp.zeros((H * K,), dtype=jnp.float32)
        lim_o = 0.1 * np.sqrt(6.0 / (C + C))
        out_w = jax.random.uniform(k4, (C, C), dtype=jnp.float32, minval=-lim_o, maxval=lim_o)
        return {'x': x, 'wave_w': wave_w, 'wave_b': wave_b, 'kernel_w': kernel_w, 'kernel_b': kernel_b, 'out_w': out_w}
    _L0_attn_in = _L0_attn_setup()

    def _L0_ffn_setup():
        import jax, jax.numpy as jnp
        import numpy as np
        TOP_K = 2
        key = jax.random.key(seed)
        k1, k2, k3, k4 = jax.random.split(key, 4)
        B, T, D, H, E = (2, 256, 128, 256, 8)
        x = jax.random.normal(k1, (B, T, D), dtype=jnp.float32)
        w12 = jax.random.normal(k2, (E, 2 * H, D), dtype=jnp.float32) * D ** (-0.5)
        w3 = jax.random.normal(k3, (E, D, H), dtype=jnp.float32) * H ** (-0.5)
        gate_w = jax.random.normal(k4, (E, D), dtype=jnp.float32) * D ** (-0.5)
        return {'x': x, 'w12': w12, 'w3': w3, 'gate_w': gate_w}
    _L0_ffn_in = _L0_ffn_setup()
    _L0_c = _w((lambda *s: np.random.randn(*s).astype(np.float32) * 0.05)(16, 128))
    _L0_wmod = _w((lambda *s: np.random.randn(*s).astype(np.float32) * 0.05)(128, 6 * 128) * 128 ** (-0.5))
    _d = {'L0_attn_x': _L0_attn_in['x'], 'L0_attn_wave_w': _L0_attn_in['wave_w'], 'L0_attn_wave_b': _L0_attn_in['wave_b'], 'L0_attn_kernel_w': _L0_attn_in['kernel_w'], 'L0_attn_kernel_b': _L0_attn_in['kernel_b'], 'L0_attn_out_w': _L0_attn_in['out_w'], 'L0_ffn_w12': _L0_ffn_in['w12'], 'L0_ffn_w3': _L0_ffn_in['w3'], 'L0_ffn_gate_w': _L0_ffn_in['gate_w'], 'L0_c': _L0_c, 'L0_wmod': _L0_wmod}
    _x0 = _d['L0_attn_x']
    _d['L0_attn_x'] = jax.random.normal(jax.random.fold_in(jax.random.key(seed), 1), (16, 512, 128), dtype=_x0.dtype)
    del _x0
    return _d

def reference(L0_attn_x, L0_attn_wave_w, L0_attn_wave_b, L0_attn_kernel_w, L0_attn_kernel_b, L0_attn_out_w, L0_ffn_w12, L0_ffn_w3, L0_ffn_gate_w, L0_c, L0_wmod):

    def _L0_attn_ref(x, wave_w, wave_b, kernel_w, kernel_b, out_w):
        import jax, jax.numpy as jnp
        import numpy as np
        C = 128
        H = 8
        MAX_SAMPLES = 32
        HALF_S = MAX_SAMPLES // 2
        S = 2 * HALF_S
        K = 64
        MAX_FREQ = 16.0
        MIN_FREQ = 1.0
        MAX_RECEPTIVE = HALF_S * MAX_FREQ
        B, L = (2, 128)

        def _gather_conv(x, wave_w, wave_b, kernel_w, kernel_b, out_w):
            Bx, Lx, Cx = x.shape
            D = Cx // H
            wave = (x @ wave_w.T + wave_b).reshape(Bx, Lx, H, 2)
            freq = MIN_FREQ + jax.nn.sigmoid(wave[..., 0]) * (MAX_FREQ - MIN_FREQ)
            phase = jnp.tanh(wave[..., 1]) * freq
            taps = jnp.arange(S, dtype=x.dtype) - HALF_S + 0.5
            offs = phase[..., None] + freq[..., None] * taps
            pos = jnp.arange(Lx, dtype=x.dtype)[None, :, None, None] + offs
            pos = jnp.clip(pos, 0.0, Lx - 1)
            i0f = jnp.floor(pos)
            frac = pos - i0f
            i0 = i0f.astype(jnp.int32)
            i1 = jnp.minimum(i0 + 1, Lx - 1)
            xh = x.reshape(Bx, Lx, H, D)
            b_idx = jnp.arange(Bx)[:, None, None, None]
            h_idx = jnp.arange(H)[None, None, :, None]
            g0 = xh[b_idx, i0, h_idx]
            g1 = xh[b_idx, i1, h_idx]
            gathered = g0 + frac[..., None] * (g1 - g0)
            kmat = (x @ kernel_w.T + kernel_b).reshape(Bx, Lx, H, K)
            bins = jnp.clip(jnp.floor((offs + MAX_RECEPTIVE) / (2.0 * MAX_RECEPTIVE) * K).astype(jnp.int32), 0, K - 1)
            w = jnp.take_along_axis(kmat, bins, axis=3)
            y = jnp.einsum('blhs,blhsd->blhd', w, gathered).reshape(Bx, Lx, Cx)
            return y @ out_w.T
        return _gather_conv(x, wave_w, wave_b, kernel_w, kernel_b, out_w)

    def _L0_ffn_ref(x, w12, w3, gate_w):
        import jax, jax.numpy as jnp
        import numpy as np
        TOP_K = 2
        E = gate_w.shape[0]
        H = w3.shape[-1]
        scores = jnp.einsum('btd,ed->bte', x, gate_w)
        topk_scores, topk_idx = jax.lax.top_k(scores, TOP_K)
        topk_probs = jax.nn.softmax(topk_scores, axis=-1)
        total_probs = jnp.sum(jax.nn.one_hot(topk_idx, E, dtype=topk_probs.dtype) * topk_probs[..., None], axis=-2)
        h12 = jnp.einsum('btd,ehd->bteh', x, w12)
        h1, h2 = (h12[..., :H], h12[..., H:])
        hidden = jax.nn.silu(h1) * h2
        expert_out = jnp.einsum('bteh,edh->bted', hidden, w3)
        y = jnp.sum(total_probs[..., None] * expert_out, axis=-2)
        return y
    x = L0_attn_x
    mod = (_silu(L0_c) @ L0_wmod).reshape(L0_c.shape[0], 6, 1, -1)
    sa, ca, ga, sb, cb, gb = (mod[:, 0], mod[:, 1], mod[:, 2], mod[:, 3], mod[:, 4], mod[:, 5])
    ga = (2 * (ga >= 0) - 1) * jnp.maximum(jnp.abs(ga), 0.25)
    gb = (2 * (gb >= 0) - 1) * jnp.maximum(jnp.abs(gb), 0.25)
    h = _layernorm(x, axis=-1) * (1 + ca) + sa
    x = x + ga * _L0_attn_ref(h, L0_attn_wave_w, L0_attn_wave_b, L0_attn_kernel_w, L0_attn_kernel_b, L0_attn_out_w)
    h = _layernorm(x, axis=-1) * (1 + cb) + sb
    x = x + gb * _L0_ffn_ref(h, L0_ffn_w12, L0_ffn_w3, L0_ffn_gate_w)
    return x

_drawn_inputs = setup_inputs


def setup_inputs(seed=0):
    import zlib

    import numpy as np

    out = dict(_drawn_inputs(seed))
    spreads = {'L0_attn_wave_b': (0.0, 0.4), 'L0_attn_kernel_b': (0.0, 0.51)}
    factors = {'L0_attn_wave_w': 3.895, 'L0_attn_kernel_w': 5.724, 'L0_attn_out_w': 3.312}
    for name, (base, spread) in spreads.items():
        noise = np.random.default_rng([zlib.crc32(name.encode()), seed]).standard_normal(out[name].shape)
        drawn = base * np.exp(spread * noise) if base else spread * noise
        out[name] = jnp.asarray(drawn.astype(out[name].dtype))
    for name, factor in factors.items():
        out[name] = (out[name] * factor).astype(out[name].dtype)
    return out
```

```python
import concourse.bass as bass
from concourse import mybir
from contextlib import ExitStack

B, L, C = 16, 512, 128
HEADS, D, TAPS, BINS = 8, 16, 32, 64
P = 128
RES = 8
HP = 64
PAIRS = B // 2
NX = L + RES
NG = NX // 8
KROW = BINS + 4
KALL = HEADS * KROW
KLD = KALL + 1
DO = D + 1
NJ = L // P
TILES = RES * HEADS
UNIT = 2 ** 19
EXPERTS, FF = 8, 256
HALVES = FF // P
NTOK = 512
RPT = NTOK // P
EPS = 1e-5
MAX_FREQ, MIN_FREQ = 16.0, 1.0


def build(nc, x, wave_wT, wave_b, kern_wT, kern_b, out_wT, w12T, w3T, gateT, cT, wmod,
          c_rel, c_bin, c_tok, c_ident, c_iota, out):
    fp32, i32, u32 = mybir.dt.float32, mybir.dt.int32, mybir.dt.uint32
    ALU, ACT, AX = mybir.AluOpType, mybir.ActivationFunctionType, mybir.AxisListType

    def rows(ap, extra):
        return bass.AP(ap.tensor, ap.offset, [list(ap.ap[0])] + [list(e) for e in extra])

    xflat = x.rearrange("b l c -> (b l c)").rearrange("(i p n) -> p i n", i=PAIRS, p=P)
    oflat = out.rearrange("b l c -> (b l c)").rearrange("(i p n) -> i p n", i=PAIRS, p=P)
    modscr = nc.dram_tensor("mod_scratch", [B, 6 * C], fp32, kind="Internal")
    hscr = nc.dram_tensor("h_scratch", [PAIRS, 2 * L * C], fp32, kind="Internal")
    kscr = nc.dram_tensor("k_scratch", [PAIRS, RES, P * KALL], fp32, kind="Internal")

    ctx = ExitStack()
    with ctx:
        def sb(name, shape, dt=fp32):
            return ctx.enter_context(nc.sbuf_tensor(name, shape, dt))

        def pb(name):
            return ctx.enter_context(nc.psum_tensor(name, [P, 512], fp32))

        def sem(name):
            return ctx.enter_context(nc.semaphore(name))

        rel = sb("rel", [P, NX])
        binpos = sb("binpos", [P, BINS - 1])
        tokpos = sb("tokpos", [P, RES])
        ident = sb("ident", [P, P])
        iota = sb("iota", [P, EXPERTS])
        kw = sb("kw", [P, HEADS * BINS])
        kbias = sb("kbias", [P, HEADS * BINS])
        ww = sb("ww", [P, 2 * HEADS])
        wbias = sb("wbias", [P, 2 * HEADS])
        ow = sb("ow", [P, C])
        w12 = sb("w12", [P, EXPERTS * 2 * FF])
        w3 = sb("w3", [P, EXPERTS * HALVES, C])
        gw = sb("gw", [P, EXPERTS])
        ct = sb("ct", [P, B])
        cs = sb("cs", [P, B])
        wm = sb("wm", [P, 6 * C])
        mod = sb("mod", [B, 6 * C])
        msign = sb("msign", [B, C])
        mabs = sb("mabs", [B, C])
        xs = sb("xs", [P, PAIRS, RES * C])
        xc = sb("xc", [P, RES, C])
        mb = sb("mb", [P, 6, C])
        stats = sb("stats", [P, RES, 6])
        mv = sb("mv", [P, RES, 2])
        var = sb("var", [P, RES])
        std = sb("std", [P, RES])
        rstd = sb("rstd", [P, RES])
        rtmp = sb("rtmp", [P, RES])
        hn = sb("hn", [P, RES, C])
        ht = sb("ht", [P, RES, P])
        hjr = sb("hjr", [P, 2 * NJ, C])
        hj = sb("hj", [P, 2 * NJ, HEADS * DO])
        hedge = sb("hedge", [P, 2, C])
        wv = sb("wv", [P, RES, 2 * HEADS])
        freq = sb("freq", [P, RES, HEADS])
        shift = sb("shift", [P, RES, HEADS])
        inv = sb("inv", [P, RES, HEADS])
        pscale = sb("pscale", [P, RES, HEADS])
        pbias = sb("pbias", [P, RES, HEADS])
        dcap = sb("dcap", [P, RES, HEADS])
        ufloor = sb("ufloor", [P, RES, HEADS])
        negf = sb("negf", [P, RES, HEADS])
        left = sb("left", [P, RES, HEADS])
        wtot = sb("wtot", [P, RES, HEADS])
        kn = sb("kn", [P, 2, HEADS, KROW])
        kdiff = sb("kdiff", [P, HEADS, BINS - 1])
        vq = sb("vq", [P, HEADS, BINS - 1])
        vq2 = sb("vq2", [P, HEADS, BINS - 1])
        tq = sb("tq", [P, HEADS, BINS - 1], i32)
        tq2 = sb("tq2", [P, HEADS, BINS - 1], i32)
        tk = sb("tk", [P, HEADS, BINS - 1])
        red = sb("red", [P, HEADS])
        ks = sb("ks", [P, 2, KLD + 3])
        kd = sb("kd", [P, 2, HEADS, KROW])
        vt = sb("vt", [P, 2, NX])
        xt = sb("xt", [P, 2, NX], i32)
        dt_ = sb("dt", [P, 2, 2, NX], i32)
        up = sb("up", [P, 2, NX])
        gt = sb("gt", [P, NX])
        at = sb("at", [P, 2, NX])
        fx = sb("fx", [P, NG])
        fx2 = sb("fx2", [P, NG])
        att = sb("att", [P, 2, 512])
        ys = sb("ys", [P, HEADS, DO])
        clip = sb("clip", [P, HEADS])
        clipl = sb("clipl", [P, HEADS])
        clipr = sb("clipr", [P, HEADS])
        ya = sb("ya", [P, C])
        yb = sb("yb", [P, C])
        yy = sb("yy", [P, RES, C])
        sc = sb("sc", [P, RES, EXPERTS])
        top = sb("top", [P, RES, 8])
        topi = sb("topi", [P, RES, 8], u32)
        topf = sb("topf", [P, RES, 8])
        gd = sb("gd", [P, RES])
        ge = sb("ge", [P, RES])
        g1 = sb("g1", [P, RES])
        g2 = sb("g2", [P, RES])
        gden = sb("gden", [P, RES])
        oh1 = sb("oh1", [P, RES, EXPERTS])
        oh2 = sb("oh2", [P, RES, EXPERTS])
        prob = sb("prob", [P, RES, EXPERTS])
        sh = sb("sh", [P, 2, NTOK])
        hid = sb("hid", [P, 2, HALVES, NTOK])
        acc = sb("acc", [P, RES, C])
        cell = sb("cell", [P, 1])
        pcell = sb("pcell", [P, 1])

        ps = [pb(f"ps{n}") for n in range(8)]
        ps_t, ps_y, ps_f = ps[0:2], ps[2:4], [ps[4:6], ps[6:8]]

        s_const, s_mod, s_modst, s_modld = sem("consts_loaded"), sem("mod_done"), sem("mod_stored"), sem("mod_loaded")
        s_silu, s_modps = sem("silu_done"), sem("mod_product")
        s_setup = sem("ones_set")
        s_xc, s_var, s_std, s_h = sem("x_copied"), sem("variance"), sem("deviation"), sem("h_ready")
        s_hst, s_hld, s_hj = sem("h_stored"), sem("h_loaded"), sem("hj_ready")
        s_tp, s_tc = sem("transposed"), sem("transposed_copied")
        s_wps, s_wv, s_tanh, s_par = sem("wave_product"), sem("wave_biased"), sem("tanh_done"), sem("params_ready")
        s_kps, s_kn, s_kst = sem("k_product"), sem("k_ready"), [sem(f"k_stored{n}") for n in range(2)]
        s_vq, s_w = sem("bin_v_ready"), sem("tap_counts_read")
        s_ksl, s_ksu, s_kd = [sem(f"ks_loaded{n}") for n in range(2)], sem("ks_used"), sem("kdiff_ready")
        s_v, s_cl, s_d, s_up, s_g, s_a = sem("v_ready"), sem("v_clamped"), sem("fractions_ready"), sem("up_ready"), sem("up_used"), sem("a_ready")
        s_at, s_atc, s_y = sem("a_transposed"), sem("a_copied"), sem("y_product")
        s_yu, s_yy = sem("y_read"), sem("y_ready")
        s_op, s_gp, s_gc, s_gd, s_ge = sem("out_product"), sem("gate_product"), sem("gate_used"), sem("gap_ready"), sem("gap_exp")
        s_f, s_si, s_hid, s_e, s_ac = sem("ff_product"), sem("silu_ready"), sem("hidden_ready"), sem("expert_product"), sem("expert_added")
        s_o, s_out, s_ch = sem("out_ready"), sem("out_stored"), sem("dve_step")
        s_end = sem("pass_done")

        consts = [(rel[:], c_rel), (binpos[:], c_bin), (tokpos[:], c_tok), (ident[:], c_ident), (iota[:], c_iota),
                  (kw[:], kern_wT), (ww[:], wave_wT), (ow[:], out_wT), (gw[:], gateT),
                  (ct[:], cT), (wm[:], wmod), (w12[:], w12T), (w3[:], w3T.rearrange("k p c -> p k c"))]
        for dst, src, n in ((kbias, kern_b, HEADS * BINS), (wbias, wave_b, 2 * HEADS)):
            consts.append((dst[:], bass.AP(src.tensor, src.offset, [[0, P], [1, n]])))
        NCONST = 16 * (len(consts) + PAIRS)
        NLN = RES + 1

        block = ctx.enter_context(nc.Block())

        @block.sync
        def _(sp):
            for dst, src in consts:
                sp.dma_start(dst, src).then_inc(s_const, 16)
            for i in range(PAIRS):
                sp.dma_start(xs[:, i, :], xflat[:, i, :]).then_inc(s_const, 16)
            sp.wait_ge(s_mod, 2)
            sp.dma_start(modscr[:, :], mod[:, :]).then_inc(s_modst, 16)
            sp.wait_ge(s_modst, 16)
            with sp.Fori(0, PAIRS) as i:
                def pinned(ap):
                    return bass.AP(ap.tensor, sp.snap(ap.offset), [list(e) for e in ap.ap])

                row = [modscr[bass.ds(2 * i + b, 1), :] for b in range(2)]
                row = [pinned(bass.AP(a.tensor, a.offset, [[0, HP], [1, 6 * C]])) for a in row]
                hall = hscr[bass.ds(i, 1), :]
                hst = pinned(hall.rearrange("o (p n) -> (o p) n", p=P))
                hin = pinned(hall.rearrange("o (q j c) -> (o j) q c", q=2 * NJ, j=P))
                edges = [(b, e, pinned(bass.AP(hall.tensor, hall.offset + (b * L + tok) * C, [[0, HP], [1, C]])))
                         for b in range(2) for e, tok in ((0, 0), (1, L - 1))]
                sp.wait_ge(s_end, sp.snap(2 * i + 2))
                for b in range(2):
                    sp.dma_start(mb[HP * b:HP * b + HP, :, :].rearrange("p a c -> p (a c)"), row[b]).then_inc(s_modld, 16)
                n_h, n_hst = sp.snap(i + 1), sp.snap(16 * i + 16)
                sp.wait_ge(s_h, n_h)
                sp.dma_start(hst, hn[:, :, :].rearrange("p r c -> p (r c)")).then_inc(s_hst, 16)
                sp.wait_ge(s_hst, n_hst)
                sp.dma_start(hjr[:, :, :], hin).then_inc(s_hld, 16)
                for b, e, src in edges:
                    sp.dma_start(hedge[HP * b:HP * b + HP, e, :], src).then_inc(s_hld, 16)
                for r in range(RES):
                    dst = pinned(kscr[bass.ds(i, 1), r, :].rearrange("o (p n) -> (o p) n", p=P))
                    sp.wait_ge(s_kn, sp.snap(RES * i + r + 1))
                    sp.dma_start(dst, kn[:, r % 2, :, :].rearrange("p h k -> p (h k)")).then_inc(s_kst[r % 2], 16)
                n_kst = sp.snap(8 * RES * (i + 1))
                for r in range(RES):
                    kr = kscr[bass.ds(i, 1), r, :]
                    src = [pinned(bass.AP(kr.tensor, kr.offset + b * HP * KALL + BINS // 2, [[KALL - 1, HP], [1, KLD]])) for b in range(2)]
                    if r == 0:
                        for parity in s_kst:
                            sp.wait_ge(parity, n_kst)
                    if r >= 2:
                        sp.wait_ge(s_ksu, sp.snap(RES * i + r - 1))
                    for b in range(2):
                        sp.dma_start(ks[HP * b:HP * b + HP, r % 2, 0:KLD], src[b]).then_inc(s_ksl[r % 2], 16)
                dst = pinned(oflat[bass.ds(i, 1), :, :].rearrange("o p n -> (o p) n"))
                sp.wait_ge(s_o, sp.snap(i + 1))
                sp.dma_start(dst, xc[:, :, :].rearrange("p r c -> p (r c)")).then_inc(s_out, 16)
            sp.wait_ge(s_out, 16 * PAIRS)

        @block.gpsimd
        def _(pool):
            c_one = ident[:, 0:1]
            pool.wait_ge(s_const, NCONST)
            for q in range(2 * NJ):
                pool.memset(rows(hj[:, q, D:D + 1], [[DO, HEADS]]), 1.0).then_inc(s_setup, 1)
            pool.wait_ge(s_setup, 2 * NJ)
            with pool.Fori(0, PAIRS) as i:
                pool.wait_ge(s_end, 2 * i + 2)
                pool.wait_ge(s_hld, 80 * (i + 1))
                pool.tensor_tensor(pcell[:, :], c_one, c_one, ALU.mult)
                for q in range(2 * NJ):
                    pool.tensor_copy(hj[:, q, :].rearrange("p (h d) -> p h d", d=DO)[:, :, 0:D],
                                     hjr[:, q, :].rearrange("p (h d) -> p h d", d=D)).then_inc(s_hj, 1)
                for r in range(RES):
                    if r >= 1:
                        pool.wait_ge(s_w, RES * i + r)
                    else:
                        pool.wait_ge(s_par, i + 1)
                    pool.wait_ge(s_kn, RES * i + r + 1)
                    pool.tensor_tensor(vq[:, :, :], rows(binpos[:, :], [[0, HEADS], [1, BINS - 1]]),
                                       rows(pscale[:, r, :], [[1, HEADS], [0, BINS - 1]]), ALU.mult).then_inc(s_vq, 1)
                    pool.tensor_tensor(kdiff[:, :, :], kn[:, r % 2, :, 3:2 + BINS],
                                       kn[:, r % 2, :, 2:1 + BINS], ALU.subtract).then_inc(s_vq, 1)
                    pool.wait_ge(s_vq, 3 * (RES * i + r) + 2)
                    pool.tensor_tensor(vq2[:, :, :], vq[:, :, :],
                                       rows(pbias[:, r, :], [[1, HEADS], [0, BINS - 1]]), ALU.add).then_inc(s_vq, 1)

        @block.scalar
        def _(act):
            act.wait_ge(s_const, NCONST)
            act.activation(cs[:, :], ct[:, :], ACT.Silu).then_inc(s_silu, 1)
            act.wait_ge(s_modps, 2)
            for n in range(2):
                act.activation(mod[:, n * 384:n * 384 + 384], ps[n][0:B, 0:384], ACT.Copy).then_inc(s_silu, 1)
            with act.Fori(0, PAIRS) as i:
                act.wait_ge(s_end, 2 * i + 2)
                act.activation(xc[:, :, :].rearrange("p r c -> p (r c)"), xs[:, bass.ds(i, 1), :].rearrange("p o n -> p (o n)"),
                               ACT.Copy).then_inc(s_xc, 1)
                act.wait_ge(s_var, 2 * i + 1)
                act.activation(std[:, :], var[:, :], ACT.Sqrt).then_inc(s_std, 1)
                for n in range(2):
                    act.wait_ge(s_tp, 6 * i + n + 1)
                    act.activation(ht[:, 4 * n:4 * n + 4, :].rearrange("p r t -> p (r t)"), ps_t[n][:, :], ACT.Copy).then_inc(s_tc, 1)
                act.wait_ge(s_wv, i + 1)
                act.activation(freq[:, :, :], rows(wv[:, 0, 0:1], [[2, TILES]]), ACT.Tanh, scale=0.5).then_inc(s_tanh, 1)
                act.activation(shift[:, :, :], rows(wv[:, 0, 1:2], [[2, TILES]]), ACT.Tanh).then_inc(s_tanh, 1)
                act.wait_ge(s_par, i + 1)

                def scaled(t):
                    r, h = t // HEADS, t % HEADS
                    if t >= 2:
                        act.wait_ge(s_cl, 2 * (TILES * i + t - 1))
                    act.activation(vt[:, t % 2, :], rel[:, :], ACT.Identity, bias=pbias[:, r, h:h + 1],
                                   scale=pscale[:, r, h:h + 1]).then_inc(s_v, 1)

                def copied(t):
                    act.wait_ge(s_at, TILES * i + t + 1)
                    if t >= 2:
                        act.wait_ge(s_y, TILES * i + t - 1)
                    act.activation(att[:, t % 2, :], ps_t[t % 2][:, :], ACT.Copy).then_inc(s_atc, 1)

                scaled(0)
                scaled(1)
                for t in range(TILES):
                    r, h = t // HEADS, t % HEADS
                    act.wait_ge(s_d, TILES * i + t + 1)
                    if t >= 2:
                        act.wait_ge(s_g, TILES * i + t - 1)
                    act.activation(up[:, t % 2, :], dt_[:, t % 2, 0, :], ACT.Relu, bias=ufloor[:, r, h:h + 1]).then_inc(s_up, 1)
                    if t + 2 < TILES:
                        scaled(t + 2)
                    if t >= 1:
                        copied(t - 1)
                copied(TILES - 1)
                for n in range(2):
                    act.wait_ge(s_tp, 6 * i + 2 + n + 1)
                    act.activation(ht[:, 4 * n:4 * n + 4, :].rearrange("p r t -> p (r t)"), ps_t[n][:, :], ACT.Copy).then_inc(s_tc, 1)
                act.wait_ge(s_var, 2 * i + 2)
                act.activation(std[:, :], var[:, :], ACT.Sqrt).then_inc(s_std, 1)
                for n in range(2):
                    act.wait_ge(s_tp, 6 * i + 4 + n + 1)
                    act.activation(ht[:, 4 * n:4 * n + 4, :].rearrange("p r t -> p (r t)"), ps_t[n][:, :], ACT.Copy).then_inc(s_tc, 1)
                act.wait_ge(s_gd, i + 1)
                act.activation(ge[:, :], gd[:, :], ACT.Exp).then_inc(s_ge, 1)
                for u in range(2 * EXPERTS * HALVES):
                    act.wait_ge(s_f, 32 * i + u + 1)
                    if u >= 2:
                        act.wait_ge(s_hid, 32 * i + u - 1)
                    act.activation(sh[:, u % 2, :], ps_f[u % 2][0][:, :], ACT.Silu).then_inc(s_si, 1)

        @block.tensor
        def _(pe):
            pe.wait_ge(s_silu, 1)
            for n in range(2):
                nc.tensor.matmul(ps[n][0:B, 0:384], cs[:, :], wm[:, n * 384:n * 384 + 384], start=True, stop=True).then_inc(s_modps, 1)
            pe.wait_ge(s_silu, 3)
            with pe.Fori(0, PAIRS) as i:
                def turned(src, n):
                    for r in range(4):
                        last = nc.tensor.transpose(ps_t[n][:, r * P:r * P + P], src[:, 4 * n + r, :], ident[:, :])
                    last.then_inc(s_tp, 1)

                pe.wait_ge(s_h, i + 1)
                for n in range(2):
                    turned(hn, n)
                pe.wait_ge(s_tc, 6 * i + 2)
                for r in range(RES):
                    last = nc.tensor.matmul(ps_f[1][1][:, r * 16:r * 16 + 16], ht[:, r, :], ww[:, :], start=True, stop=True)
                last.then_inc(s_wps, 1)
                for r in range(RES):
                    if r >= 2:
                        pe.wait_ge(s_kn, RES * i + r - 1)
                    nc.tensor.matmul(ps_y[r % 2][:, :], ht[:, r, :], kw[:, :], start=True, stop=True).then_inc(s_kps, 1)
                pe.wait_ge(s_kn, RES * (i + 1))
                pe.wait_ge(s_hj, 2 * NJ * (i + 1))

                def weigh(t):
                    r, h = t // HEADS, t % HEADS
                    pe.wait_ge(s_atc, TILES * i + t + 1)
                    if h == 0 and r >= 2:
                        pe.wait_ge(s_yu, RES * i + r - 1)
                    for b in range(2):
                        for j in range(NJ):
                            last = nc.tensor.matmul(ps_y[r % 2][HP * b:HP * b + HP, h * DO:h * DO + DO],
                                                    att[:, t % 2, j * P + HP * b:j * P + HP * b + HP],
                                                    hj[:, b * NJ + j, h * DO:h * DO + DO], start=(j == 0), stop=(j == NJ - 1))
                    last.then_inc(s_y, 1)

                for t in range(TILES):
                    r = t // HEADS
                    pe.wait_ge(s_a, TILES * i + t + 1)
                    if t >= 2:
                        pe.wait_ge(s_atc, TILES * i + t - 1)
                    for j in range(NJ):
                        o = RES - r + j * P
                        last = nc.tensor.transpose(ps_t[t % 2][:, j * P:j * P + P], at[:, t % 2, o:o + P], ident[:, :])
                    last.then_inc(s_at, 1)
                    if t >= 1:
                        weigh(t - 1)
                weigh(TILES - 1)
                pe.wait_ge(s_yy, RES * (i + 1))
                for n in range(2):
                    turned(yy, n)
                pe.wait_ge(s_tc, 6 * i + 4)
                for r in range(RES):
                    last = nc.tensor.matmul(ps_y[r // 4][:, (r % 4) * C:(r % 4) * C + C], ht[:, r, :], ow[:, :], start=True, stop=True)
                last.then_inc(s_op, 1)
                pe.wait_ge(s_gc, i + 1)
                for n in range(2):
                    turned(hn, n)
                pe.wait_ge(s_tc, 6 * i + 6)
                for r in range(RES):
                    last = nc.tensor.matmul(ps_t[0][:, r * 8:r * 8 + 8], ht[:, r, :], gw[:, :], start=True, stop=True)
                last.then_inc(s_gp, 1)

                def raised(u):
                    q, e, k = u // 16, u // 2 % EXPERTS, u % 2
                    if u >= 2:
                        pe.wait_ge(s_hid, 32 * i + u - 1)
                    for part in range(2):
                        o = e * 2 * FF + part * FF + k * P
                        last = nc.tensor.matmul(ps_f[u % 2][part][:, :], w12[:, o:o + P],
                                                ht[:, RPT * q:RPT * q + RPT, :].rearrange("p r t -> p (r t)"), start=True, stop=True)
                    last.then_inc(s_f, 1)

                def lowered(v):
                    e = v % EXPERTS
                    pe.wait_ge(s_hid, 32 * i + 2 * v + 2)
                    if v >= 2:
                        pe.wait_ge(s_ac, 64 * i + RPT * (v - 1))
                    for m in range(RPT):
                        for k in range(HALVES):
                            last = nc.tensor.matmul(ps_y[v % 2][:, m * C:m * C + C], hid[:, v % 2, k, m * P:m * P + P],
                                                    w3[:, e * HALVES + k, :], start=(k == 0), stop=(k == HALVES - 1))
                    last.then_inc(s_e, 1)

                raised(0)
                raised(1)
                for v in range(2 * EXPERTS):
                    if v + 1 < 2 * EXPERTS:
                        raised(2 * v + 2)
                        raised(2 * v + 3)
                    lowered(v)
                pe.wait_ge(s_o, i + 1)

        CHAIN = chain_len()

        @block.vector
        def _(dve):
            n = [0]
            base = [0]

            def link(ins):
                n[0] += 1
                ins.then_inc(s_ch, 1)
                dve.wait_ge(s_ch, base[0] + n[0])

            def fence():
                nc.vector.memset(cell[:, :], 0.0)

            dve.wait_ge(s_silu, 3)
            for a in (1, 4):
                link(nc.vector.tensor_scalar(mod[:, a * C:a * C + C], mod[:, a * C:a * C + C], 1.0, None, ALU.add))
            for a in (2, 5):
                g = mod[:, a * C:a * C + C]
                nc.vector.tensor_scalar(msign[:, :], g, 0.0, 2.0, ALU.is_ge, ALU.mult)
                link(nc.vector.scalar_tensor_tensor(mabs[:, :], g, -1.0, g, ALU.mult, ALU.max))
                link(nc.vector.tensor_scalar(mabs[:, :], mabs[:, :], 0.25, None, ALU.max))
                link(nc.vector.tensor_scalar(msign[:, :], msign[:, :], -1.0, None, ALU.add))
                nc.vector.tensor_tensor(g, msign[:, :], mabs[:, :], ALU.mult).then_inc(s_mod, 1)
                dve.wait_ge(s_mod, 1 if a == 2 else 2)
            setup = n[0]
            nc.vector.memset(cell[:, :], 0.0).then_inc(s_end, 2)

            with dve.Fori(0, PAIRS) as i:
                n[0] = 0
                base[0] = CHAIN * i + setup
                T0 = TILES * i

                def normed(which, scale, bias, first, done):
                    for r in range(RES):
                        ins = nc.vector.bn_stats(stats[:, r, :], xc[:, r, :])
                    link(ins)
                    fence()
                    for r in range(RES):
                        ins = nc.vector.bn_aggr(mv[:, r, :], stats[:, r, :])
                    link(ins)
                    nc.vector.tensor_scalar(var[:, :], rows(mv[:, 0, 1:2], [[2, RES]]), EPS, None, ALU.add).then_inc(s_var, 1)
                    dve.wait_ge(s_std, 2 * i + which + 1)
                    link(nc.vector.reciprocal(rstd[:, :], std[:, :]))
                    link(nc.vector.tensor_tensor(rtmp[:, :], rstd[:, :], rstd[:, :], ALU.mult))
                    link(nc.vector.tensor_tensor(rtmp[:, :], rtmp[:, :], var[:, :], ALU.mult))
                    link(nc.vector.tensor_scalar(rtmp[:, :], rtmp[:, :], -0.5, 1.5, ALU.mult, ALU.add))
                    link(nc.vector.tensor_tensor(rstd[:, :], rstd[:, :], rtmp[:, :], ALU.mult))
                    for r in range(RES):
                        ins = nc.vector.tensor_scalar(hn[:, r, :], xc[:, r, :], mv[:, r, 0:1], rstd[:, r:r + 1], ALU.subtract, ALU.mult)
                    link(ins)
                    link(nc.vector.tensor_tensor(hn[:, :, :], hn[:, :, :], rows(mb[:, scale, :], [[0, RES], [1, C]]), ALU.mult))
                    nc.vector.tensor_tensor(hn[:, :, :], hn[:, :, :], rows(mb[:, bias, :], [[0, RES], [1, C]]), ALU.add).then_inc(done, 1)

                dve.wait_ge(s_xc, i + 1)
                dve.wait_ge(s_modld, 32 * (i + 1))
                normed(0, 1, 0, True, s_h)

                dve.wait_ge(s_wps, i + 1)
                nc.vector.tensor_tensor(wv[:, :, :], ps_f[1][1][:, 0:RES * 16].rearrange("p (r w) -> p r w", w=16),
                                        rows(wbias[:, :], [[0, RES], [1, 2 * HEADS]]), ALU.add).then_inc(s_wv, 1)
                dve.wait_ge(s_tanh, 2 * (i + 1))
                half = (MAX_FREQ - MIN_FREQ) / 2
                link(nc.vector.tensor_scalar(freq[:, :, :], freq[:, :, :], half, MIN_FREQ + half, ALU.mult, ALU.add))
                link(nc.vector.reciprocal(inv[:, :, :], freq[:, :, :]))
                nc.vector.tensor_tensor(left[:, :, :], freq[:, :, :], shift[:, :, :], ALU.mult)
                link(nc.vector.tensor_scalar(pscale[:, :, :], inv[:, :, :], float(UNIT), None, ALU.mult))
                nc.vector.tensor_scalar(pbias[:, :, :], shift[:, :, :], -float(UNIT), 15.5 * UNIT - 1, ALU.mult, ALU.add)
                nc.vector.tensor_scalar(dcap[:, :, :], pscale[:, :, :], -1.0, None, ALU.add)
                link(nc.vector.tensor_scalar(negf[:, :, :], freq[:, :, :], -1.0 / UNIT, None, ALU.mult))
                nc.vector.tensor_scalar(ufloor[:, :, :], pscale[:, :, :], -float(UNIT - 1), 0.0, ALU.add, ALU.min)
                link(nc.vector.tensor_tensor(left[:, :, :], left[:, :, :], rows(tokpos[:, :], [[1, RES], [0, HEADS]]), ALU.add))
                nc.vector.tensor_scalar(left[:, :, :], left[:, :, :], L / 2.0, None, ALU.is_lt).then_inc(s_par, 1)

                for r in range(RES):
                    dve.wait_ge(s_kps, RES * i + r + 1)
                    if r >= 2:
                        dve.wait_ge(s_kst[r % 2], 16 * (RES // 2 * i + r // 2))
                        dve.wait_ge(s_vq, 3 * (RES * i + r - 1))
                    link(nc.vector.tensor_tensor(kn[:, r % 2, :, 2:2 + BINS], ps_y[r % 2][:, :].rearrange("p (h k) -> p h k", k=BINS),
                                                 kbias[:, :].rearrange("p (h k) -> p h k", k=BINS), ALU.add))
                    nc.vector.tensor_copy(kn[:, r % 2, :, 0:2], rows(kn[:, r % 2, 0, 2:3], [[KROW, HEADS], [0, 2]]))
                    nc.vector.tensor_copy(kn[:, r % 2, :, 2 + BINS:KROW], rows(kn[:, r % 2, 0, 1 + BINS:2 + BINS], [[KROW, HEADS], [0, 2]])).then_inc(s_kn, 1)
                    dve.wait_ge(s_vq, 3 * (RES * i + r + 1))
                    link(nc.vector.tensor_scalar(tq[:, :, :], vq2[:, :, :], -1.0, float(TAPS * UNIT - 1), ALU.max, ALU.min))
                    link(nc.vector.tensor_scalar(tq2[:, :, :], tq[:, :, :], 19, None, ALU.arith_shift_right))
                    link(nc.vector.scalar_tensor_tensor(tk[:, :, :], tq2[:, :, :], 1.0, kdiff[:, :, :], ALU.add, ALU.mult))
                    link(nc.vector.reduce_sum(red[:, :], tk[:, :, :], AX.X))
                    nc.vector.scalar_tensor_tensor(wtot[:, r, :], rows(kn[:, r % 2, 0, 1 + BINS:2 + BINS], [[KROW, HEADS]]), float(TAPS), red[:, :],
                                                   ALU.mult, ALU.subtract).then_inc(s_w, 1)

                def fractions(t):
                    r = t // HEADS
                    dve.wait_ge(s_v, T0 + t + 1)
                    if t >= 2:
                        dve.wait_ge(s_up, T0 + t - 1)
                    nc.vector.tensor_scalar(xt[:, 0, :], vt[:, t % 2, :], -float(UNIT), float((TAPS - 1) * UNIT), ALU.max, ALU.min).then_inc(s_cl, 1)
                    nc.vector.tensor_scalar(xt[:, 1, :], vt[:, t % 2, :], -1.0, float(TAPS * UNIT - 1), ALU.max, ALU.min).then_inc(s_cl, 1)
                    dve.wait_ge(s_cl, 2 * (T0 + t + 1))
                    nc.vector.tensor_scalar(dt_[:, t % 2, :, :], xt[:, :, :], UNIT - 1, None, ALU.bitwise_and).then_inc(s_d, 1)

                def combined(r):
                    dve.wait_ge(s_y, T0 + HEADS * (r + 1))
                    nc.vector.tensor_tensor(ys[:, :, :], ps_y[r % 2][:, 0:HEADS * DO].rearrange("p (h d) -> p h d", d=DO),
                                            rows(negf[:, r, :], [[1, HEADS], [0, DO]]), ALU.mult).then_inc(s_yu, 1)
                    dve.wait_ge(s_yu, RES * i + r + 1)
                    link(nc.vector.tensor_tensor(clip[:, :], wtot[:, r, :], rows(ys[:, 0, D:D + 1], [[DO, HEADS]]), ALU.subtract))
                    link(nc.vector.tensor_tensor(clipl[:, :], clip[:, :], left[:, r, :], ALU.mult))
                    link(nc.vector.tensor_tensor(clipr[:, :], clip[:, :], clipl[:, :], ALU.subtract))
                    v = [a[:, :].rearrange("p (h d) -> p h d", d=D) for a in (ya, yb)]
                    nc.vector.tensor_tensor(v[0], hedge[:, 0, :].rearrange("p (h d) -> p h d", d=D), rows(clipl[:, :], [[1, HEADS], [0, D]]), ALU.mult)
                    link(nc.vector.tensor_tensor(v[1], hedge[:, 1, :].rearrange("p (h d) -> p h d", d=D), rows(clipr[:, :], [[1, HEADS], [0, D]]), ALU.mult))
                    link(nc.vector.tensor_tensor(ya[:, :], ya[:, :], yb[:, :], ALU.add))
                    nc.vector.tensor_tensor(yy[:, r, :].rearrange("p (h d) -> p h d", d=D), v[0], ys[:, :, 0:D], ALU.add).then_inc(s_yy, 1)

                dve.wait_ge(s_hld, 80 * (i + 1))
                fractions(0)
                for t in range(TILES):
                    r, h = t // HEADS, t % HEADS
                    if h == 0:
                        dve.wait_ge(s_ksl[r % 2], 32 * (RES // 2 * i + r // 2 + 1))
                        link(nc.vector.tensor_tensor(kd[:, r % 2, :, 0:NG], rows(ks[:, r % 2, 0:1], [[KROW, HEADS], [1, NG]]),
                                                     rows(ks[:, r % 2, 1:2], [[KROW, HEADS], [1, NG]]), ALU.subtract))
                    if t + 1 < TILES:
                        fractions(t + 1)
                    down = dt_[:, t % 2, 1, :]
                    cap = dcap[:, r, h:h + 1]
                    dve.wait_ge(s_up, T0 + t + 1)
                    nc.vector.scalar_tensor_tensor(gt[:, :], down, cap, up[:, t % 2, :], ALU.min, ALU.subtract).then_inc(s_g, 1)
                    link(nc.vector.tensor_scalar(fx[:, :], rows(dt_[:, t % 2, 1, 0:1], [[8, NG]]), cap, cap, ALU.min, ALU.subtract))
                    nc.vector.tensor_tensor(fx2[:, :], fx[:, :], kd[:, r % 2, h, 0:NG], ALU.mult)
                    if t >= 2:
                        dve.wait_ge(s_at, T0 + t - 1)
                    ins = (nc.vector.scalar_tensor_tensor(at[:, t % 2, :].rearrange("p (g k) -> p g k", k=8), gt[:, :].rearrange("p (g k) -> p g k", k=8), cap,
                                                        rows(ks[:, r % 2, 1 + h * KROW:2 + h * KROW], [[1, NG], [0, 8]]), ALU.subtract, ALU.mult))
                    if h == HEADS - 1:
                        ins.then_inc(s_ksu, 1)
                        dve.wait_ge(s_ksu, RES * i + r + 1)
                    else:
                        link(ins)
                    a0 = rows(at[:, t % 2, 0:1], [[8, NG]])
                    ins = nc.vector.tensor_tensor(a0, a0, fx2[:, :], ALU.add)
                    ins.then_inc(s_a, 1)
                    dve.wait_ge(s_a, T0 + t + 1)
                    if h == 2 and r >= 1:
                        combined(r - 1)
                combined(RES - 1)

                dve.wait_ge(s_op, i + 1)
                for m in range(2):
                    o = ps_y[m][:, :].rearrange("p (r c) -> p r c", c=C)
                    link(nc.vector.tensor_tensor(hn[:, 4 * m:4 * m + 4, :], o, rows(mb[:, 2, :], [[0, 4], [1, C]]), ALU.mult))
                link(nc.vector.tensor_tensor(xc[:, :, :], xc[:, :, :], hn[:, :, :], ALU.add))
                normed(1, 4, 3, False, s_gc)

                dve.wait_ge(s_gp, i + 1)
                link(nc.vector.tensor_copy(sc[:, :, :], ps_t[0][:, 0:RES * 8].rearrange("p (r e) -> p r e", e=8)))
                fence()
                for r in range(RES):
                    ins = nc.vector.max(top[:, r, :], sc[:, r, :])
                link(ins)
                fence()
                for r in range(RES):
                    ins = nc.vector.max_index(topi[:, r, :], top[:, r, :], sc[:, r, :])
                link(ins)
                nc.vector.tensor_tensor(gd[:, :], rows(top[:, 0, 1:2], [[8, RES]]), rows(top[:, 0, 0:1], [[8, RES]]), ALU.subtract).then_inc(s_gd, 1)
                link(nc.vector.tensor_copy(topf[:, :, :], topi[:, :, :]))
                it = rows(iota[:, :], [[0, RES], [1, EXPERTS]])
                nc.vector.tensor_tensor(oh1[:, :, :], it, rows(topf[:, 0, 0:1], [[8, RES], [0, EXPERTS]]), ALU.is_equal)
                nc.vector.tensor_tensor(oh2[:, :, :], it, rows(topf[:, 0, 1:2], [[8, RES], [0, EXPERTS]]), ALU.is_equal)
                dve.wait_ge(s_ge, i + 1)
                link(nc.vector.tensor_scalar(gden[:, :], ge[:, :], 1.0, None, ALU.add))
                link(nc.vector.reciprocal(g1[:, :], gden[:, :]))
                link(nc.vector.tensor_tensor(g2[:, :], g1[:, :], ge[:, :], ALU.mult))
                nc.vector.tensor_tensor(oh1[:, :, :], oh1[:, :, :], rows(g1[:, :], [[1, RES], [0, EXPERTS]]), ALU.mult)
                link(nc.vector.tensor_tensor(oh2[:, :, :], oh2[:, :, :], rows(g2[:, :], [[1, RES], [0, EXPERTS]]), ALU.mult))
                link(nc.vector.tensor_tensor(prob[:, :, :], oh1[:, :, :], oh2[:, :, :], ALU.add))

                def hidden(u):
                    q, v = u // 16, u // 2
                    dve.wait_ge(s_si, 32 * i + u + 1)
                    if v >= 2:
                        dve.wait_ge(s_e, 16 * i + v - 1)
                    nc.vector.tensor_tensor(hid[:, v % 2, u % 2, :], sh[:, u % 2, :], ps_f[u % 2][1][:, :], ALU.mult).then_inc(s_hid, 1)

                hidden(0)
                hidden(1)
                for v in range(2 * EXPERTS):
                    q, e = v // EXPERTS, v % EXPERTS
                    if v + 1 < 2 * EXPERTS:
                        hidden(2 * v + 2)
                        hidden(2 * v + 3)
                    dve.wait_ge(s_e, 16 * i + v + 1)
                    if e:
                        dve.wait_ge(s_ac, 64 * i + RPT * v)
                    for m in range(RPT):
                        r = q * RPT + m
                        o = ps_y[v % 2][:, m * C:m * C + C]
                        if e == 0:
                            nc.vector.tensor_scalar(acc[:, r, :], o, prob[:, r, 0:1], None, ALU.mult).then_inc(s_ac, 1)
                        else:
                            nc.vector.scalar_tensor_tensor(acc[:, r, :], o, prob[:, r, e:e + 1], acc[:, r, :], ALU.mult, ALU.add).then_inc(s_ac, 1)
                dve.wait_ge(s_ac, 64 * (i + 1))
                link(nc.vector.tensor_tensor(acc[:, :, :], acc[:, :, :], rows(mb[:, 5, :], [[0, RES], [1, C]]), ALU.mult))
                nc.vector.tensor_tensor(xc[:, :, :], xc[:, :, :], acc[:, :, :], ALU.add).then_inc(s_o, 1)
                dve.wait_ge(s_out, 16 * (i + 1))
                nc.vector.memset(cell[:, :], 0.0).then_inc(s_end, 2)
                assert n[0] == CHAIN, n[0]


def chain_len():
    norm = 2 + 5 + 2
    params = 5
    bins = RES * 5
    tiles = TILES * 2
    combine = RES * 5
    tail = 3
    gate = 3 + 1 + 3 + 2
    return 2 * norm + params + bins + tiles + combine + tail + gate + 1


def kernel(**inputs):
    import numpy as np
    import concourse.bacc as bacc
    from concourse.bass_utils import run_bass_kernel_spmd as run

    f = np.float32
    g = {k: np.asarray(v) for k, v in inputs.items()}
    p, xcol = np.arange(P), np.arange(NX)
    tok = 8 * (p % HP)
    arrays = {
        "x": g["L0_attn_x"],
        "wave_wT": g["L0_attn_wave_w"].T, "wave_b": g["L0_attn_wave_b"],
        "kern_wT": g["L0_attn_kernel_w"].T, "kern_b": g["L0_attn_kernel_b"],
        "out_wT": g["L0_attn_out_w"].T,
        "w12T": g["L0_ffn_w12"].reshape(EXPERTS * 2 * FF, C).T,
        "w3T": g["L0_ffn_w3"].transpose(0, 2, 1).reshape(EXPERTS * HALVES, P, C),
        "gateT": g["L0_ffn_gate_w"].T, "cT": g["L0_c"].T, "wmod": g["L0_wmod"],
        "c_rel": (xcol[None, :] - 8 - tok[:, None]).astype(f),
        "c_bin": np.broadcast_to(8 * np.arange(1, BINS) - L // 2, (P, BINS - 1)).astype(f),
        "c_tok": (tok[:, None] + np.arange(RES)[None, :]).astype(f),
        "c_ident": np.eye(P, dtype=f),
        "c_iota": np.broadcast_to(np.arange(EXPERTS), (P, EXPERTS)).astype(f),
    }
    nc = bacc.Bacc("TRN2", target_bir_lowering=False, num_devices=1)
    data, args = {}, []
    for name, a in arrays.items():
        a = np.ascontiguousarray(a)
        data[f"in_{name}"] = a
        args.append(nc.dram_tensor(f"in_{name}", a.shape, mybir.dt.from_np(a.dtype), kind="ExternalInput").ap())
    args.append(nc.dram_tensor("out_0", (B, L, C), mybir.dt.float32, kind="ExternalOutput").ap())
    build(nc, *args)
    r = run(nc, [data], core_ids=[0])
    return r.results[0]["out_0"]
```

```python
import concourse.bass as bass
from concourse import mybir
from contextlib import ExitStack

B, L, C = 16, 512, 128
HEADS, D, TAPS, BINS = 8, 16, 32, 64
P = 128
RES = 8
HP = 64
PAIRS = B // 2
NX = L + RES
NG = NX // 8
KROW = BINS + 4
KALL = HEADS * KROW
NV = NX + 2
DO = D + 1
NJ = L // P
TILES = RES * HEADS
UNIT = 2 ** 19
EXPERTS, FF = 8, 256
HALVES = FF // P
NTOK = 512
RPT = NTOK // P
EPS = 1e-5
MAX_FREQ, MIN_FREQ = 16.0, 1.0


def build(nc, x, wave_wT, wave_b, kern_wT, kern_b, out_wT, w12T, w3T, gateT, cT, wmod,
          c_rel, c_bin, c_tok, c_ident, c_iota, out):
    fp32, i32, u32 = mybir.dt.float32, mybir.dt.int32, mybir.dt.uint32
    ALU, ACT, AX = mybir.AluOpType, mybir.ActivationFunctionType, mybir.AxisListType

    def rows(ap, extra):
        return bass.AP(ap.tensor, ap.offset, [list(ap.ap[0])] + [list(e) for e in extra])

    xflat = x.rearrange("b l c -> (b l c)").rearrange("(i p n) -> p i n", i=PAIRS, p=P)
    oflat = out.rearrange("b l c -> (b l c)").rearrange("(i p n) -> i p n", i=PAIRS, p=P)
    modscr = nc.dram_tensor("mod_scratch", [B, 6 * C], fp32, kind="Internal")
    hscr = nc.dram_tensor("h_scratch", [PAIRS, 2 * L * C], fp32, kind="Internal")
    kscr = nc.dram_tensor("k_scratch", [PAIRS, RES, P * KALL], fp32, kind="Internal")

    ctx = ExitStack()
    with ctx:
        def sb(name, shape, dt=fp32):
            return ctx.enter_context(nc.sbuf_tensor(name, shape, dt))

        def pb(name):
            return ctx.enter_context(nc.psum_tensor(name, [P, 512], fp32))

        def sem(name):
            return ctx.enter_context(nc.semaphore(name))

        rel = sb("rel", [P, NV])
        binpos = sb("binpos", [P, BINS - 1])
        tokpos = sb("tokpos", [P, RES])
        ident = sb("ident", [P, P])
        iota = sb("iota", [P, EXPERTS])
        kw = sb("kw", [P, HEADS * BINS])
        kbias = sb("kbias", [P, HEADS * BINS])
        ww = sb("ww", [P, 2 * HEADS])
        wbias = sb("wbias", [P, 2 * HEADS])
        ow = sb("ow", [P, C])
        w12 = sb("w12", [P, EXPERTS * 2 * FF])
        w3 = sb("w3", [P, EXPERTS * HALVES, C])
        gw = sb("gw", [P, EXPERTS])
        ct = sb("ct", [P, B])
        cs = sb("cs", [P, B])
        wm = sb("wm", [P, 6 * C])
        mod = sb("mod", [B, 6 * C])
        msign = sb("msign", [B, C])
        mabs = sb("mabs", [B, C])
        xs = sb("xs", [P, PAIRS, RES * C])
        xc = sb("xc", [P, RES, C])
        mb = sb("mb", [P, 6, C])
        stats = sb("stats", [P, RES, 6])
        mv = sb("mv", [P, RES, 2])
        var = sb("var", [P, RES])
        std = sb("std", [P, RES])
        rstd = sb("rstd", [P, RES])
        rtmp = sb("rtmp", [P, RES])
        hn = sb("hn", [P, RES, C])
        ht = sb("ht", [P, RES, P])
        h2t = sb("h2t", [P, RES, P])
        xo = sb("xo", [P, RES, C])
        gb = sb("gb", [P, C])
        hjr = sb("hjr", [P, 2 * NJ, C])
        hj = sb("hj", [P, 2 * NJ, HEADS * DO])
        hedge = sb("hedge", [P, 2, C])
        wv = sb("wv", [P, RES, 2 * HEADS])
        freq = sb("freq", [P, RES, HEADS])
        shift = sb("shift", [P, RES, HEADS])
        inv = sb("inv", [P, RES, HEADS])
        pscale = sb("pscale", [P, RES, HEADS])
        pbias = sb("pbias", [P, RES, HEADS])
        dcap = sb("dcap", [P, RES, HEADS])
        ufloor = sb("ufloor", [P, RES, HEADS])
        posf = sb("posf", [P, RES, HEADS])
        left = sb("left", [P, RES, HEADS])
        wtot = sb("wtot", [P, RES, HEADS])
        kn = sb("kn", [P, 2, HEADS, KROW])
        kdiff = sb("kdiff", [P, 2, HEADS, BINS - 1])
        vq = sb("vq", [P, HEADS, BINS - 1])
        vq2 = sb("vq2", [P, 2, HEADS, BINS - 1])
        tq = sb("tq", [P, HEADS, BINS - 1], i32)
        tq2 = sb("tq2", [P, HEADS, BINS - 1], i32)
        tk = sb("tk", [P, HEADS, BINS - 1])
        red = sb("red", [P, HEADS])
        ks = sb("ks", [P, 2, KALL])
        vt = sb("vt", [P, 2, NV])
        xt = sb("xt", [P, 2, NV], i32)
        frac = sb("frac", [P, 2, 2, NV], i32)
        up = sb("up", [P, 2, NX])
        down = sb("down", [P, 2, NX])
        aup = sb("aup", [P, 2, NX])
        adown = sb("adown", [P, 2, NX])
        att = sb("att", [P, 2, 512])
        ys = sb("ys", [P, HEADS, DO])
        clip = sb("clip", [P, HEADS])
        clipl = sb("clipl", [P, HEADS])
        clipr = sb("clipr", [P, HEADS])
        ya = sb("ya", [P, C])
        yb = sb("yb", [P, C])
        yy = sb("yy", [P, RES, C])
        sc = sb("sc", [P, RES, EXPERTS])
        top = sb("top", [P, RES, 8])
        topi = sb("topi", [P, RES, 8], u32)
        topf = sb("topf", [P, RES, 8])
        gd = sb("gd", [P, RES])
        ge = sb("ge", [P, RES])
        g1 = sb("g1", [P, RES])
        g2 = sb("g2", [P, RES])
        gden = sb("gden", [P, RES])
        oh1 = sb("oh1", [P, RES, EXPERTS])
        oh2 = sb("oh2", [P, RES, EXPERTS])
        prob = sb("prob", [P, RES, EXPERTS])
        sh = sb("sh", [P, 2, NTOK])
        hid = sb("hid", [P, 2, HALVES, NTOK])
        acc = sb("acc", [P, RES, C])
        cell = sb("cell", [P, 1])
        pcell = sb("pcell", [P, 1])

        ps = [pb(f"ps{n}") for n in range(8)]
        ps_t, ps_k, ps_y, ps_e, ps_f = ps[0:2], ps[2:4], ps[2], ps[3], [ps[4:6], ps[6:8]]

        s_const, s_mod, s_modst, s_modld = sem("consts_loaded"), sem("mod_done"), sem("mod_stored"), sem("mod_loaded")
        s_silu, s_modps = sem("silu_done"), sem("mod_product")
        s_setup = sem("ones_set")
        s_xc, s_var, s_std, s_h = sem("x_copied"), sem("variance"), sem("deviation"), sem("h_ready")
        s_hst, s_hld, s_hj = sem("h_stored"), sem("h_loaded"), sem("hj_ready")
        s_tp, s_tc = sem("transposed"), sem("transposed_copied")
        s_wps, s_wv, s_tanh, s_par = sem("wave_product"), sem("wave_biased"), sem("tanh_done"), sem("params_ready")
        s_kps, s_kn, s_kst = sem("k_product"), sem("k_ready"), [sem(f"k_stored{n}") for n in range(2)]
        s_vq, s_kdf, s_w = sem("bin_v_ready"), sem("bin_steps_ready"), sem("tap_counts_read")
        s_ksl = [sem(f"ks_loaded{n}") for n in range(2)]
        s_v, s_cl, s_d, s_up, s_down = sem("v_ready"), sem("v_clamped"), sem("fractions_ready"), sem("up_ready"), sem("down_ready")
        s_aup, s_adown = sem("up_weighted"), sem("down_weighted")
        s_at, s_atc, s_y = sem("a_transposed"), sem("a_copied"), sem("y_product")
        s_yu, s_yy = sem("y_read"), sem("y_ready")
        s_op, s_gp, s_gc, s_gd, s_ge = sem("out_product"), sem("gate_product"), sem("gate_used"), sem("gap_ready"), sem("gap_exp")
        s_f, s_si, s_hid, s_e, s_ac = sem("ff_product"), sem("silu_ready"), sem("hidden_ready"), sem("expert_product"), sem("expert_added")
        s_o, s_out, s_ch = sem("out_ready"), sem("out_stored"), sem("dve_step")
        s_end, s_fin = sem("pass_done"), sem("experts_gated")
        LAST = TILES + 4

        consts = [(rel[:], c_rel), (binpos[:], c_bin), (tokpos[:], c_tok), (ident[:], c_ident), (iota[:], c_iota),
                  (kw[:], kern_wT), (ww[:], wave_wT), (ow[:], out_wT), (gw[:], gateT),
                  (ct[:], cT), (wm[:], wmod), (w12[:], w12T), (w3[:], w3T.rearrange("k p c -> p k c"))]
        for dst, src, n in ((kbias, kern_b, HEADS * BINS), (wbias, wave_b, 2 * HEADS)):
            consts.append((dst[:], bass.AP(src.tensor, src.offset, [[0, P], [1, n]])))
        NCONST = 16 * (len(consts) + PAIRS)
        NLN = RES + 1

        block = ctx.enter_context(nc.Block())

        @block.sync
        def _(sp):
            for dst, src in consts:
                sp.dma_start(dst, src).then_inc(s_const, 16)
            for i in range(PAIRS):
                sp.dma_start(xs[:, i, :], xflat[:, i, :]).then_inc(s_const, 16)
            sp.wait_ge(s_mod, 2)
            sp.dma_start(modscr[:, :], mod[:, :]).then_inc(s_modst, 16)
            sp.wait_ge(s_modst, 16)
            def snap(v):
                return v if isinstance(v, int) else sp.snap(v)

            def pinned(ap):
                return bass.AP(ap.tensor, snap(ap.offset), [list(e) for e in ap.ap])

            def pair(i):
                row = [modscr[bass.ds(2 * i + b, 1), :] for b in range(2)]
                row = [pinned(bass.AP(a.tensor, a.offset, [[0, HP], [1, 6 * C]])) for a in row]
                hall = hscr[bass.ds(i, 1), :]
                hst = pinned(hall.rearrange("o (p n) -> (o p) n", p=P))
                hin = pinned(hall.rearrange("o (q j c) -> (o j) q c", q=2 * NJ, j=P))
                edges = [(b, e, pinned(bass.AP(hall.tensor, hall.offset + (b * L + tok) * C, [[0, HP], [1, C]])))
                         for b in range(2) for e, tok in ((0, 0), (1, L - 1))]
                sp.wait_ge(s_end, snap(2 * i + 2))
                for b in range(2):
                    sp.dma_start(mb[HP * b:HP * b + HP, :, :].rearrange("p a c -> p (a c)"), row[b]).then_inc(s_modld, 16)
                n_h, n_hst = snap(i + 1), snap(16 * i + 16)
                sp.wait_ge(s_h, n_h)
                sp.dma_start(hst, hn[:, :, :].rearrange("p r c -> p (r c)")).then_inc(s_hst, 16)
                sp.wait_ge(s_hst, n_hst)
                sp.dma_start(hjr[:, :, :], hin).then_inc(s_hld, 16)
                for b, e, src in edges:
                    sp.dma_start(hedge[HP * b:HP * b + HP, e, :], src).then_inc(s_hld, 16)
                for r in range(RES):
                    dst = pinned(kscr[bass.ds(i, 1), r, :].rearrange("o (p n) -> (o p) n", p=P))
                    sp.wait_ge(s_kn, snap(RES * i + r + 1))
                    sp.dma_start(dst, kn[:, r % 2, :, :].rearrange("p h k -> p (h k)")).then_inc(s_kst[r % 2], 16)
                n_kst = snap(8 * RES * (i + 1))
                for r in range(RES):
                    kr = kscr[bass.ds(i, 1), r, :]
                    src = [pinned(bass.AP(kr.tensor, kr.offset + b * HP * KALL + BINS // 2 + 1, [[KALL - 1, HP], [1, KALL]])) for b in range(2)]
                    if r == 0:
                        for parity in s_kst:
                            sp.wait_ge(parity, n_kst)
                    if r >= 2:
                        sp.wait_ge(s_adown, snap(TILES * i + HEADS * (r - 1)))
                    for b in range(2):
                        sp.dma_start(ks[HP * b:HP * b + HP, r % 2, :], src[b]).then_inc(s_ksl[r % 2], 16)
                if not (isinstance(i, int) and i == 0):
                    store(i - 1)

            def store(f):
                dst = pinned(oflat[bass.ds(f, 1), :, :].rearrange("o p n -> (o p) n"))
                sp.wait_ge(s_o, snap(f + 1))
                sp.dma_start(dst, xo[:, :, :].rearrange("p r c -> p (r c)")).then_inc(s_out, 16)

            pair(0)
            with sp.Fori(1, PAIRS) as i:
                pair(i)
            store(PAIRS - 1)
            sp.wait_ge(s_out, 16 * PAIRS)

        @block.gpsimd
        def _(pool):
            c_one = ident[:, 0:1]
            pool.wait_ge(s_const, NCONST)
            for q in range(2 * NJ):
                pool.memset(rows(hj[:, q, D:D + 1], [[DO, HEADS]]), 1.0).then_inc(s_setup, 1)
            pool.wait_ge(s_setup, 2 * NJ)
            def pair(i):
                pool.wait_ge(s_end, 2 * i + 2)
                pool.wait_ge(s_hld, 80 * (i + 1))
                pool.tensor_tensor(pcell[:, :], c_one, c_one, ALU.mult)
                for q in range(2 * NJ):
                    pool.tensor_copy(hj[:, q, :].rearrange("p (h d) -> p h d", d=DO)[:, :, 0:D],
                                     hjr[:, q, :].rearrange("p (h d) -> p h d", d=D)).then_inc(s_hj, 1)
                pool.wait_ge(s_par, i + 1)
                for r in range(RES):
                    if r >= 2:
                        pool.wait_ge(s_w, RES * i + r - 1)
                    if r >= 1:
                        pool.wait_ge(s_vq, 2 * (RES * i + r))
                    pool.tensor_tensor(vq[:, :, :], rows(binpos[:, :], [[0, HEADS], [1, BINS - 1]]),
                                       rows(pscale[:, r, :], [[1, HEADS], [0, BINS - 1]]), ALU.mult).then_inc(s_vq, 1)
                    pool.wait_ge(s_vq, 2 * (RES * i + r) + 1)
                    pool.tensor_tensor(vq2[:, r % 2, :, :], vq[:, :, :],
                                       rows(pbias[:, r, :], [[1, HEADS], [0, BINS - 1]]), ALU.add).then_inc(s_vq, 1)
                    pool.wait_ge(s_kn, RES * i + r + 1)
                    pool.tensor_tensor(kdiff[:, r % 2, :, :], kn[:, r % 2, :, 3:2 + BINS],
                                       kn[:, r % 2, :, 2:1 + BINS], ALU.subtract).then_inc(s_kdf, 1)

            pair(0)
            with pool.Fori(1, PAIRS) as i:
                pair(i)

        @block.scalar
        def _(act):
            act.wait_ge(s_const, NCONST)
            act.activation(cs[:, :], ct[:, :], ACT.Silu).then_inc(s_silu, 1)
            act.wait_ge(s_modps, 2)
            for n in range(2):
                act.activation(mod[:, n * 384:n * 384 + 384], ps[n][0:B, 0:384], ACT.Copy).then_inc(s_silu, 1)
            def gated(f, t):
                u = (t - 1) // 2
                if t % 2 == 1 and u < 2 * EXPERTS * HALVES:
                    act.wait_ge(s_f, 32 * f + u + 1)
                    if u >= 2:
                        act.wait_ge(s_hid, 32 * f + u - 1)
                    act.activation(sh[:, u % 2, :], ps_f[u % 2][0][:, :], ACT.Silu).then_inc(s_si, 1)

            def pair(i, experts):
                act.wait_ge(s_end, 2 * i + 2)
                act.activation(xc[:, :, :].rearrange("p r c -> p (r c)"), xs[:, bass.ds(i, 1), :].rearrange("p o n -> p (o n)"),
                               ACT.Copy).then_inc(s_xc, 1)
                act.wait_ge(s_var, 2 * i + 1)
                act.activation(std[:, :], var[:, :], ACT.Sqrt).then_inc(s_std, 1)
                for n in range(2):
                    act.wait_ge(s_tp, 6 * i + n + 1)
                    act.activation(ht[:, 4 * n:4 * n + 4, :].rearrange("p r t -> p (r t)"), ps_t[n][:, :], ACT.Copy).then_inc(s_tc, 1)
                act.wait_ge(s_wv, i + 1)
                act.activation(freq[:, :, :], rows(wv[:, 0, 0:1], [[2, TILES]]), ACT.Tanh, scale=0.5).then_inc(s_tanh, 1)
                act.activation(shift[:, :, :], rows(wv[:, 0, 1:2], [[2, TILES]]), ACT.Tanh).then_inc(s_tanh, 1)
                act.wait_ge(s_par, i + 1)

                def scaled(t):
                    r, h = t // HEADS, t % HEADS
                    if t >= 2:
                        act.wait_ge(s_cl, 2 * (TILES * i + t - 1))
                    act.activation(vt[:, t % 2, :], rel[:, :], ACT.Identity, bias=pbias[:, r, h:h + 1],
                                   scale=pscale[:, r, h:h + 1]).then_inc(s_v, 1)

                def copied(t):
                    act.wait_ge(s_at, TILES * i + t + 1)
                    if t >= 2:
                        act.wait_ge(s_y, TILES * i + t - 1)
                    act.activation(att[:, t % 2, :], ps_t[t % 2][:, :], ACT.Copy).then_inc(s_atc, 1)

                scaled(0)
                scaled(1)
                for t in range(TILES):
                    r, h = t // HEADS, t % HEADS
                    act.wait_ge(s_d, TILES * i + t + 1)
                    if t >= 2:
                        act.wait_ge(s_aup, TILES * i + t - 1)
                    act.activation(up[:, t % 2, :], frac[:, t % 2, 0, 0:NX], ACT.Relu, bias=ufloor[:, r, h:h + 1]).then_inc(s_up, 1)
                    if t >= 2:
                        act.wait_ge(s_adown, TILES * i + t - 1)
                    act.activation(down[:, t % 2, :], frac[:, t % 2, 1, 1:NX + 1], ACT.Relu, bias=dcap[:, r, h:h + 1], scale=-1.0).then_inc(s_down, 1)
                    if t + 2 < TILES:
                        scaled(t + 2)
                    if t >= 1:
                        copied(t - 1)
                    if experts:
                        gated(i - 1, t)
                copied(TILES - 1)
                for n in range(2):
                    act.wait_ge(s_tp, 6 * i + 2 + n + 1)
                    act.activation(ht[:, 4 * n:4 * n + 4, :].rearrange("p r t -> p (r t)"), ps_t[n][:, :], ACT.Copy).then_inc(s_tc, 1)
                act.wait_ge(s_var, 2 * i + 2)
                act.activation(std[:, :], var[:, :], ACT.Sqrt).then_inc(s_std, 1)
                for n in range(2):
                    act.wait_ge(s_tp, 6 * i + 4 + n + 1)
                    act.activation(h2t[:, 4 * n:4 * n + 4, :].rearrange("p r t -> p (r t)"), ps_t[n][:, :], ACT.Copy).then_inc(s_tc, 1)
                act.wait_ge(s_gd, i + 1)
                act.activation(ge[:, :], gd[:, :], ACT.Exp).then_inc(s_ge, 1)

            pair(0, False)
            with act.Fori(1, PAIRS) as i:
                pair(i, True)
            for t in range(LAST):
                gated(PAIRS - 1, t)

        @block.tensor
        def _(pe):
            pe.wait_ge(s_silu, 1)
            for n in range(2):
                nc.tensor.matmul(ps[n][0:B, 0:384], cs[:, :], wm[:, n * 384:n * 384 + 384], start=True, stop=True).then_inc(s_modps, 1)
            pe.wait_ge(s_silu, 3)
            def pair(i, experts):
                def turned(src, n):
                    for r in range(4):
                        last = nc.tensor.transpose(ps_t[n][:, r * P:r * P + P], src[:, 4 * n + r, :], ident[:, :])
                    last.then_inc(s_tp, 1)

                pe.wait_ge(s_h, i + 1)
                for n in range(2):
                    turned(hn, n)
                pe.wait_ge(s_tc, 6 * i + 2)
                for r in range(RES):
                    last = nc.tensor.matmul(ps_f[1][1][:, r * 16:r * 16 + 16], ht[:, r, :], ww[:, :], start=True, stop=True)
                last.then_inc(s_wps, 1)
                for r in range(RES):
                    if r >= 2:
                        pe.wait_ge(s_kn, RES * i + r - 1)
                    nc.tensor.matmul(ps_k[r % 2][:, :], ht[:, r, :], kw[:, :], start=True, stop=True).then_inc(s_kps, 1)
                pe.wait_ge(s_kn, RES * (i + 1))
                pe.wait_ge(s_hj, 2 * NJ * (i + 1))

                def weigh(t):
                    r, h = t // HEADS, t % HEADS
                    pe.wait_ge(s_atc, TILES * i + t + 1)
                    if h == 0 and r >= 1:
                        pe.wait_ge(s_yu, RES * i + r)
                    for b in range(2):
                        for j in range(NJ):
                            last = nc.tensor.matmul(ps_y[HP * b:HP * b + HP, h * DO:h * DO + DO],
                                                    att[:, t % 2, j * P + HP * b:j * P + HP * b + HP],
                                                    hj[:, b * NJ + j, h * DO:h * DO + DO], start=(j == 0), stop=(j == NJ - 1))
                    last.then_inc(s_y, 1)

                for t in range(TILES):
                    r = t // HEADS
                    pe.wait_ge(s_aup, TILES * i + t + 1)
                    pe.wait_ge(s_adown, TILES * i + t + 1)
                    if t >= 2:
                        pe.wait_ge(s_atc, TILES * i + t - 1)
                    for j in range(NJ):
                        o = RES - r + j * P
                        dst = ps_t[t % 2][:, j * P:j * P + P]
                        nc.tensor.matmul(dst, aup[:, t % 2, o:o + P], ident[:, :], is_transpose=True, start=True, stop=False)
                        last = nc.tensor.matmul(dst, adown[:, t % 2, o - 1:o - 1 + P], ident[:, :], is_transpose=True, start=False, stop=True)
                    last.then_inc(s_at, 1)
                    if t >= 1:
                        weigh(t - 1)
                    if experts:
                        experts_step(i - 1, t)
                weigh(TILES - 1)
                if experts:
                    for t in range(TILES, LAST):
                        experts_step(i - 1, t)
                pe.wait_ge(s_yy, RES * (i + 1))
                for n in range(2):
                    turned(yy, n)
                pe.wait_ge(s_tc, 6 * i + 4)
                for r in range(RES):
                    last = nc.tensor.matmul(ps_k[r // 4][:, (r % 4) * C:(r % 4) * C + C], ht[:, r, :], ow[:, :], start=True, stop=True)
                last.then_inc(s_op, 1)
                pe.wait_ge(s_gc, i + 1)
                for n in range(2):
                    turned(hn, n)
                pe.wait_ge(s_tc, 6 * i + 6)
                for r in range(RES):
                    last = nc.tensor.matmul(ps_t[0][:, r * 8:r * 8 + 8], h2t[:, r, :], gw[:, :], start=True, stop=True)
                last.then_inc(s_gp, 1)

            def experts_step(f, t):
                u, v = t // 2, (t - 5) // 4
                if t % 2 == 0 and u < 2 * EXPERTS * HALVES:
                    q, e, k = u // 16, u // 2 % EXPERTS, u % 2
                    if u >= 2:
                        pe.wait_ge(s_hid, 32 * f + u - 1)
                    for part in range(2):
                        o = e * 2 * FF + part * FF + k * P
                        last = nc.tensor.matmul(ps_f[u % 2][part][:, :], w12[:, o:o + P],
                                                h2t[:, RPT * q:RPT * q + RPT, :].rearrange("p r t -> p (r t)"), start=True, stop=True)
                    last.then_inc(s_f, 1)
                if t % 4 == 1 and 0 <= v < 2 * EXPERTS:
                    e = v % EXPERTS
                    pe.wait_ge(s_hid, 32 * f + 2 * v + 2)
                    if v >= 1:
                        pe.wait_ge(s_ac, 64 * f + RPT * v)
                    for m in range(RPT):
                        for k in range(HALVES):
                            last = nc.tensor.matmul(ps_e[:, m * C:m * C + C], hid[:, v % 2, k, m * P:m * P + P],
                                                    w3[:, e * HALVES + k, :], start=(k == 0), stop=(k == HALVES - 1))
                    last.then_inc(s_e, 1)

            pair(0, False)
            with pe.Fori(1, PAIRS) as i:
                pair(i, True)
            for t in range(LAST):
                experts_step(PAIRS - 1, t)

        CHAIN = chain_len()

        @block.vector
        def _(dve):
            n = [0]
            base = [0]

            def link(ins):
                n[0] += 1
                ins.then_inc(s_ch, 1)
                dve.wait_ge(s_ch, base[0] + n[0])

            def fence():
                nc.vector.memset(cell[:, :], 0.0)

            dve.wait_ge(s_silu, 3)
            for a in (1, 4):
                link(nc.vector.tensor_scalar(mod[:, a * C:a * C + C], mod[:, a * C:a * C + C], 1.0, None, ALU.add))
            for a in (2, 5):
                g = mod[:, a * C:a * C + C]
                nc.vector.tensor_scalar(msign[:, :], g, 0.0, 2.0, ALU.is_ge, ALU.mult)
                link(nc.vector.scalar_tensor_tensor(mabs[:, :], g, -1.0, g, ALU.mult, ALU.max))
                link(nc.vector.tensor_scalar(mabs[:, :], mabs[:, :], 0.25, None, ALU.max))
                link(nc.vector.tensor_scalar(msign[:, :], msign[:, :], -1.0, None, ALU.add))
                nc.vector.tensor_tensor(g, msign[:, :], mabs[:, :], ALU.mult).then_inc(s_mod, 1)
                dve.wait_ge(s_mod, 1 if a == 2 else 2)
            setup = n[0]
            nc.vector.memset(cell[:, :], 0.0).then_inc(s_end, 2)

            def experts_step(f, t):
                u, v = (t - 2) // 2, (t - 7) // 4
                if t % 2 == 0 and 0 <= u < 2 * EXPERTS * HALVES:
                    dve.wait_ge(s_si, 32 * f + u + 1)
                    if u >= 4:
                        dve.wait_ge(s_e, 16 * f + u // 2 - 1)
                    nc.vector.tensor_tensor(hid[:, u // 2 % 2, u % 2, :], sh[:, u % 2, :], ps_f[u % 2][1][:, :], ALU.mult).then_inc(s_hid, 1)
                if t % 4 == 3 and 0 <= v < 2 * EXPERTS:
                    q, e = v // EXPERTS, v % EXPERTS
                    dve.wait_ge(s_e, 16 * f + v + 1)
                    if e:
                        dve.wait_ge(s_ac, 64 * f + RPT * v)
                    for m in range(RPT):
                        r = q * RPT + m
                        o = ps_e[:, m * C:m * C + C]
                        if e == 0:
                            nc.vector.tensor_scalar(acc[:, r, :], o, prob[:, r, 0:1], None, ALU.mult).then_inc(s_ac, 1)
                        else:
                            nc.vector.scalar_tensor_tensor(acc[:, r, :], o, prob[:, r, e:e + 1], acc[:, r, :], ALU.mult, ALU.add).then_inc(s_ac, 1)

            def finished(f):
                dve.wait_ge(s_ac, 64 * f + 64)
                nc.vector.tensor_tensor(acc[:, :, :], acc[:, :, :], rows(gb[:, :], [[0, RES], [1, C]]), ALU.mult).then_inc(s_fin, 1)
                dve.wait_ge(s_fin, f + 1)
                nc.vector.tensor_tensor(xo[:, :, :], xo[:, :, :], acc[:, :, :], ALU.add).then_inc(s_o, 1)

            def pair(i, experts):
                n[0] = 0
                base[0] = CHAIN * i + setup
                T0 = TILES * i

                def normed(which, src, scale, bias, done):
                    for r in range(RES):
                        ins = nc.vector.bn_stats(stats[:, r, :], src[:, r, :])
                    link(ins)
                    fence()
                    for r in range(RES):
                        ins = nc.vector.bn_aggr(mv[:, r, :], stats[:, r, :])
                    link(ins)
                    nc.vector.tensor_scalar(var[:, :], rows(mv[:, 0, 1:2], [[2, RES]]), EPS, None, ALU.add).then_inc(s_var, 1)
                    dve.wait_ge(s_std, 2 * i + which + 1)
                    link(nc.vector.reciprocal(rstd[:, :], std[:, :]))
                    link(nc.vector.tensor_tensor(rtmp[:, :], rstd[:, :], rstd[:, :], ALU.mult))
                    link(nc.vector.tensor_tensor(rtmp[:, :], rtmp[:, :], var[:, :], ALU.mult))
                    link(nc.vector.tensor_scalar(rtmp[:, :], rtmp[:, :], -0.5, 1.5, ALU.mult, ALU.add))
                    link(nc.vector.tensor_tensor(rstd[:, :], rstd[:, :], rtmp[:, :], ALU.mult))
                    for r in range(RES):
                        ins = nc.vector.tensor_scalar(hn[:, r, :], src[:, r, :], mv[:, r, 0:1], rstd[:, r:r + 1], ALU.subtract, ALU.mult)
                    link(ins)
                    link(nc.vector.tensor_tensor(hn[:, :, :], hn[:, :, :], rows(mb[:, scale, :], [[0, RES], [1, C]]), ALU.mult))
                    nc.vector.tensor_tensor(hn[:, :, :], hn[:, :, :], rows(mb[:, bias, :], [[0, RES], [1, C]]), ALU.add).then_inc(done, 1)

                dve.wait_ge(s_xc, i + 1)
                dve.wait_ge(s_modld, 32 * (i + 1))
                normed(0, xc, 1, 0, s_h)

                dve.wait_ge(s_wps, i + 1)
                nc.vector.tensor_tensor(wv[:, :, :], ps_f[1][1][:, 0:RES * 16].rearrange("p (r w) -> p r w", w=16),
                                        rows(wbias[:, :], [[0, RES], [1, 2 * HEADS]]), ALU.add).then_inc(s_wv, 1)
                dve.wait_ge(s_tanh, 2 * (i + 1))
                half = (MAX_FREQ - MIN_FREQ) / 2
                link(nc.vector.tensor_scalar(freq[:, :, :], freq[:, :, :], half, MIN_FREQ + half, ALU.mult, ALU.add))
                link(nc.vector.reciprocal(inv[:, :, :], freq[:, :, :]))
                nc.vector.tensor_tensor(left[:, :, :], freq[:, :, :], shift[:, :, :], ALU.mult)
                link(nc.vector.tensor_scalar(pscale[:, :, :], inv[:, :, :], float(UNIT), None, ALU.mult))
                nc.vector.tensor_scalar(pbias[:, :, :], shift[:, :, :], -float(UNIT), 15.5 * UNIT - 1, ALU.mult, ALU.add)
                nc.vector.tensor_scalar(dcap[:, :, :], pscale[:, :, :], -1.0, None, ALU.add)
                link(nc.vector.tensor_scalar(posf[:, :, :], freq[:, :, :], 1.0 / UNIT, None, ALU.mult))
                nc.vector.tensor_scalar(ufloor[:, :, :], pscale[:, :, :], -float(UNIT - 1), 0.0, ALU.add, ALU.min)
                link(nc.vector.tensor_tensor(left[:, :, :], left[:, :, :], rows(tokpos[:, :], [[1, RES], [0, HEADS]]), ALU.add))
                nc.vector.tensor_scalar(left[:, :, :], left[:, :, :], L / 2.0, None, ALU.is_lt).then_inc(s_par, 1)

                def binned(r):
                    dve.wait_ge(s_kps, RES * i + r + 1)
                    if r >= 2:
                        dve.wait_ge(s_kst[r % 2], 16 * (RES // 2 * i + r // 2))
                        dve.wait_ge(s_kdf, RES * i + r - 1)
                        dve.wait_ge(s_w, RES * i + r - 1)
                    link(nc.vector.tensor_tensor(kn[:, r % 2, :, 2:2 + BINS], ps_k[r % 2][:, :].rearrange("p (h k) -> p h k", k=BINS),
                                                 kbias[:, :].rearrange("p (h k) -> p h k", k=BINS), ALU.add))
                    nc.vector.tensor_copy(kn[:, r % 2, :, 0:2], rows(kn[:, r % 2, 0, 2:3], [[KROW, HEADS], [0, 2]]))
                    nc.vector.tensor_copy(kn[:, r % 2, :, 2 + BINS:KROW], rows(kn[:, r % 2, 0, 1 + BINS:2 + BINS], [[KROW, HEADS], [0, 2]])).then_inc(s_kn, 1)

                binned(0)
                for r in range(RES):
                    if r + 1 < RES:
                        binned(r + 1)
                    dve.wait_ge(s_vq, 2 * (RES * i + r + 1))
                    link(nc.vector.tensor_scalar(tq[:, :, :], vq2[:, r % 2, :, :], -1.0, float(TAPS * UNIT - 1), ALU.max, ALU.min))
                    link(nc.vector.tensor_scalar(tq2[:, :, :], tq[:, :, :], 19, None, ALU.arith_shift_right))
                    dve.wait_ge(s_kdf, RES * i + r + 1)
                    link(nc.vector.scalar_tensor_tensor(tk[:, :, :], tq2[:, :, :], 1.0, kdiff[:, r % 2, :, :], ALU.add, ALU.mult))
                    link(nc.vector.reduce_sum(red[:, :], tk[:, :, :], AX.X))
                    nc.vector.scalar_tensor_tensor(wtot[:, r, :], rows(kn[:, r % 2, 0, 1 + BINS:2 + BINS], [[KROW, HEADS]]), float(TAPS), red[:, :],
                                                   ALU.mult, ALU.subtract).then_inc(s_w, 1)
                def clamped(t):
                    dve.wait_ge(s_v, T0 + t + 1)
                    if t >= 1:
                        dve.wait_ge(s_d, T0 + t)
                    nc.vector.tensor_scalar(xt[:, 0, :], vt[:, t % 2, :], -float(UNIT), float((TAPS - 1) * UNIT), ALU.max, ALU.min).then_inc(s_cl, 1)
                    nc.vector.tensor_scalar(xt[:, 1, :], vt[:, t % 2, :], -1.0, float(TAPS * UNIT - 1), ALU.max, ALU.min).then_inc(s_cl, 1)

                def fractions(t):
                    dve.wait_ge(s_cl, 2 * (T0 + t + 1))
                    if t >= 2:
                        dve.wait_ge(s_up, T0 + t - 1)
                        dve.wait_ge(s_down, T0 + t - 1)
                    nc.vector.tensor_scalar(frac[:, t % 2, :, :], xt[:, :, :], UNIT - 1, None, ALU.bitwise_and).then_inc(s_d, 1)

                def weighted(t, part, out_, ready, done):
                    r, h = t // HEADS, t % HEADS
                    dve.wait_ge(ready, T0 + t + 1)
                    if t >= 2:
                        dve.wait_ge(s_at, T0 + t - 1)
                    ins = nc.vector.tensor_tensor(out_[:, t % 2, :].rearrange("p (g k) -> p g k", k=8), part[:, t % 2, :].rearrange("p (g k) -> p g k", k=8),
                                                  rows(ks[:, r % 2, h * KROW:h * KROW + 1], [[1, NG], [0, 8]]), ALU.mult)
                    ins.then_inc(done, 1)

                def combined(r):
                    dve.wait_ge(s_y, T0 + HEADS * (r + 1))
                    nc.vector.tensor_tensor(ys[:, :, :], ps_y[:, 0:HEADS * DO].rearrange("p (h d) -> p h d", d=DO),
                                            rows(posf[:, r, :], [[1, HEADS], [0, DO]]), ALU.mult).then_inc(s_yu, 1)
                    dve.wait_ge(s_yu, RES * i + r + 1)
                    link(nc.vector.tensor_tensor(clip[:, :], wtot[:, r, :], rows(ys[:, 0, D:D + 1], [[DO, HEADS]]), ALU.subtract))
                    link(nc.vector.tensor_tensor(clipl[:, :], clip[:, :], left[:, r, :], ALU.mult))
                    link(nc.vector.tensor_tensor(clipr[:, :], clip[:, :], clipl[:, :], ALU.subtract))
                    v = [a[:, :].rearrange("p (h d) -> p h d", d=D) for a in (ya, yb)]
                    nc.vector.tensor_tensor(v[0], hedge[:, 0, :].rearrange("p (h d) -> p h d", d=D), rows(clipl[:, :], [[1, HEADS], [0, D]]), ALU.mult)
                    link(nc.vector.tensor_tensor(v[1], hedge[:, 1, :].rearrange("p (h d) -> p h d", d=D), rows(clipr[:, :], [[1, HEADS], [0, D]]), ALU.mult))
                    link(nc.vector.tensor_tensor(ya[:, :], ya[:, :], yb[:, :], ALU.add))
                    nc.vector.tensor_tensor(yy[:, r, :].rearrange("p (h d) -> p h d", d=D), v[0], ys[:, :, 0:D], ALU.add).then_inc(s_yy, 1)

                dve.wait_ge(s_hld, 80 * (i + 1))
                clamped(0)
                fractions(0)
                for t in range(TILES):
                    r, h = t // HEADS, t % HEADS
                    if t + 1 < TILES:
                        clamped(t + 1)
                    if h == 0:
                        dve.wait_ge(s_ksl[r % 2], 32 * (RES // 2 * i + r // 2 + 1))
                    weighted(t, up, aup, s_up, s_aup)
                    if t + 1 < TILES:
                        fractions(t + 1)
                    weighted(t, down, adown, s_down, s_adown)
                    if h == 1 and r >= 1:
                        combined(r - 1)
                    if experts:
                        experts_step(i - 1, t)
                if experts:
                    for t in range(TILES, LAST):
                        experts_step(i - 1, t)
                    finished(i - 1)
                    dve.wait_ge(s_out, 16 * i)
                combined(RES - 1)

                dve.wait_ge(s_op, i + 1)
                for m in range(2):
                    o = ps_k[m][:, :].rearrange("p (r c) -> p r c", c=C)
                    link(nc.vector.tensor_tensor(hn[:, 4 * m:4 * m + 4, :], o, rows(mb[:, 2, :], [[0, 4], [1, C]]), ALU.mult))
                link(nc.vector.tensor_tensor(xo[:, :, :], xc[:, :, :], hn[:, :, :], ALU.add))
                normed(1, xo, 4, 3, s_gc)

                dve.wait_ge(s_gp, i + 1)
                link(nc.vector.tensor_copy(sc[:, :, :], ps_t[0][:, 0:RES * 8].rearrange("p (r e) -> p r e", e=8)))
                fence()
                for r in range(RES):
                    ins = nc.vector.max(top[:, r, :], sc[:, r, :])
                link(ins)
                fence()
                for r in range(RES):
                    ins = nc.vector.max_index(topi[:, r, :], top[:, r, :], sc[:, r, :])
                link(ins)
                nc.vector.tensor_tensor(gd[:, :], rows(top[:, 0, 1:2], [[8, RES]]), rows(top[:, 0, 0:1], [[8, RES]]), ALU.subtract).then_inc(s_gd, 1)
                link(nc.vector.tensor_copy(topf[:, :, :], topi[:, :, :]))
                it = rows(iota[:, :], [[0, RES], [1, EXPERTS]])
                nc.vector.tensor_tensor(oh1[:, :, :], it, rows(topf[:, 0, 0:1], [[8, RES], [0, EXPERTS]]), ALU.is_equal)
                nc.vector.tensor_tensor(oh2[:, :, :], it, rows(topf[:, 0, 1:2], [[8, RES], [0, EXPERTS]]), ALU.is_equal)
                dve.wait_ge(s_ge, i + 1)
                link(nc.vector.tensor_scalar(gden[:, :], ge[:, :], 1.0, None, ALU.add))
                link(nc.vector.reciprocal(g1[:, :], gden[:, :]))
                link(nc.vector.tensor_tensor(g2[:, :], g1[:, :], ge[:, :], ALU.mult))
                nc.vector.tensor_tensor(oh1[:, :, :], oh1[:, :, :], rows(g1[:, :], [[1, RES], [0, EXPERTS]]), ALU.mult)
                link(nc.vector.tensor_tensor(oh2[:, :, :], oh2[:, :, :], rows(g2[:, :], [[1, RES], [0, EXPERTS]]), ALU.mult))
                link(nc.vector.tensor_tensor(prob[:, :, :], oh1[:, :, :], oh2[:, :, :], ALU.add))

                nc.vector.tensor_copy(gb[:, :], mb[:, 5, :]).then_inc(s_end, 2)
                assert n[0] == CHAIN, n[0]

            pair(0, False)
            with dve.Fori(1, PAIRS) as i:
                pair(i, True)
            for t in range(LAST):
                experts_step(PAIRS - 1, t)
            finished(PAIRS - 1)


def chain_len():
    norm = 2 + 5 + 2
    params = 5
    bins = RES * 5
    tiles = 0
    combine = RES * 5
    tail = 3
    gate = 3 + 1 + 3 + 2
    return 2 * norm + params + bins + tiles + combine + tail + gate


def kernel(**inputs):
    import numpy as np
    import concourse.bacc as bacc
    from concourse.bass_utils import run_bass_kernel_spmd as run

    f = np.float32
    g = {k: np.asarray(v) for k, v in inputs.items()}
    p = np.arange(P)
    tok = 8 * (p % HP)
    arrays = {
        "x": g["L0_attn_x"],
        "wave_wT": g["L0_attn_wave_w"].T, "wave_b": g["L0_attn_wave_b"],
        "kern_wT": g["L0_attn_kernel_w"].T, "kern_b": g["L0_attn_kernel_b"],
        "out_wT": g["L0_attn_out_w"].T,
        "w12T": g["L0_ffn_w12"].reshape(EXPERTS * 2 * FF, C).T,
        "w3T": g["L0_ffn_w3"].transpose(0, 2, 1).reshape(EXPERTS * HALVES, P, C),
        "gateT": g["L0_ffn_gate_w"].T, "cT": g["L0_c"].T, "wmod": g["L0_wmod"],
        "c_rel": (np.arange(NV)[None, :] - 8 - tok[:, None]).astype(f),
        "c_bin": np.broadcast_to(8 * np.arange(1, BINS) - L // 2, (P, BINS - 1)).astype(f),
        "c_tok": (tok[:, None] + np.arange(RES)[None, :]).astype(f),
        "c_ident": np.eye(P, dtype=f),
        "c_iota": np.broadcast_to(np.arange(EXPERTS), (P, EXPERTS)).astype(f),
    }
    nc = bacc.Bacc("TRN2", target_bir_lowering=False, num_devices=1)
    data, args = {}, []
    for name, a in arrays.items():
        a = np.ascontiguousarray(a)
        data[f"in_{name}"] = a
        args.append(nc.dram_tensor(f"in_{name}", a.shape, mybir.dt.from_np(a.dtype), kind="ExternalInput").ap())
    args.append(nc.dram_tensor("out_0", (B, L, C), mybir.dt.float32, kind="ExternalOutput").ap())
    build(nc, *args)
    r = run(nc, [data], core_ids=[0])
    return r.results[0]["out_0"]
```

```python
import concourse.bass as bass
from concourse import mybir
from contextlib import ExitStack

B, L, C = 16, 512, 128
HEADS, D, TAPS, BINS = 8, 16, 32, 64
P = 128
RES = 8
HP = 64
PAIRS = B // 2
NX = L + RES
NG = NX // 8
KROW = BINS + 4
KALL = HEADS * KROW
KHALF = KALL // 2
NV = NX + 2
DO = D + 1
NJ = L // P
TILES = RES * HEADS
UNIT = 2 ** 19
RING = 3
EXPERTS, FF = 8, 256
HALVES = FF // P
NTOK = 512
RPT = NTOK // P
EPS = 1e-5
MAX_FREQ, MIN_FREQ = 16.0, 1.0


def build(nc, x, wave_wT, wave_b, kern_wT, kern_b, out_wT, w12T, w3T, gateT, cT, wmod,
          c_rel, c_bin, c_tok, c_ident, c_iota, out):
    fp32, i32, u32 = mybir.dt.float32, mybir.dt.int32, mybir.dt.uint32
    ALU, ACT, AX = mybir.AluOpType, mybir.ActivationFunctionType, mybir.AxisListType

    def rows(ap, extra):
        return bass.AP(ap.tensor, ap.offset, [list(ap.ap[0])] + [list(e) for e in extra])

    xflat = x.rearrange("b l c -> (b l c)").rearrange("(i p n) -> p i n", i=PAIRS, p=P)
    oflat = out.rearrange("b l c -> (b l c)").rearrange("(i p n) -> i p n", i=PAIRS, p=P)
    modscr = nc.dram_tensor("mod_scratch", [B, 6 * C], fp32, kind="Internal")
    hscr = nc.dram_tensor("h_scratch", [PAIRS, 2 * L * C], fp32, kind="Internal")
    kscr = nc.dram_tensor("k_scratch", [PAIRS, RES, P * KALL], fp32, kind="Internal")

    ctx = ExitStack()
    with ctx:
        def sb(name, shape, dt=fp32):
            return ctx.enter_context(nc.sbuf_tensor(name, shape, dt))

        def pb(name):
            return ctx.enter_context(nc.psum_tensor(name, [P, 512], fp32))

        def sem(name):
            return ctx.enter_context(nc.semaphore(name))

        rel = sb("rel", [P, NV])
        binpos = sb("binpos", [P, BINS - 1])
        tokpos = sb("tokpos", [P, RES])
        ident = sb("ident", [P, P])
        iota = sb("iota", [P, EXPERTS])
        kw = sb("kw", [P, KALL])
        kbias = sb("kbias", [P, KALL])
        ww = sb("ww", [P, 2 * HEADS])
        wbias = sb("wbias", [P, 2 * HEADS])
        ow = sb("ow", [P, C])
        w12 = sb("w12", [P, EXPERTS * 2 * FF])
        w3 = sb("w3", [P, EXPERTS * HALVES, C])
        gw = sb("gw", [P, EXPERTS])
        ct = sb("ct", [P, B])
        cs = sb("cs", [P, B])
        mod = sb("mod", [B, 6 * C])
        msign = sb("msign", [B, C])
        mabs = sb("mabs", [B, C])
        xs = sb("xs", [P, PAIRS, RES * C])
        xc = sb("xc", [P, RES, C])
        mb = sb("mb", [P, 6, C])
        stats = sb("stats", [P, RES, 6])
        mv = sb("mv", [P, 2, RES, 2])
        var = sb("var", [P, RES])
        std = sb("std", [P, RES])
        rstd = sb("rstd", [P, 2, RES])
        mb1 = sb("mb1", [P, 2, C])
        rtmp = sb("rtmp", [P, RES])
        hn = sb("hn", [P, RES, C])
        ht = sb("ht", [P, RES, P])
        h2t = sb("h2t", [P, RES, P])
        xo = sb("xo", [P, RES, C])
        gb = sb("gb", [P, C])
        hjr = sb("hjr", [P, 2 * NJ, C])
        hj = sb("hj", [P, 2 * NJ, HEADS * DO])
        hedge = sb("hedge", [P, 2, C])
        wv = sb("wv", [P, RES, 2 * HEADS])
        freq = sb("freq", [P, RES, HEADS])
        shift = sb("shift", [P, RES, HEADS])
        inv = sb("inv", [P, RES, HEADS])
        pscale = sb("pscale", [P, RES, HEADS])
        pbias = sb("pbias", [P, RES, HEADS])
        dcap = sb("dcap", [P, RES, HEADS])
        ufloor = sb("ufloor", [P, RES, HEADS])
        posf = sb("posf", [P, RES, HEADS])
        left = sb("left", [P, RES, HEADS])
        wtot = sb("wtot", [P, RES, HEADS])
        kn = sb("kn", [P, RES, HEADS, KROW])
        kdiff = sb("kdiff", [P, 2, HEADS, BINS - 1])
        vq = sb("vq", [P, HEADS, BINS - 1])
        vq2 = sb("vq2", [P, 2, HEADS, BINS - 1])
        tq = sb("tq", [P, HEADS, BINS - 1], i32)
        tq2 = sb("tq2", [P, HEADS, BINS - 1], i32)
        tk = sb("tk", [P, HEADS, BINS - 1])
        red = sb("red", [P, HEADS])
        ks = sb("ks", [P, 2, KALL])
        vt = sb("vt", [P, 2, NV])
        xt = sb("xt", [P, 2, NV], i32)
        frac = sb("frac", [P, 2, 2, NV], i32)
        up = sb("up", [P, 2, NX])
        down = sb("down", [P, 2, NX])
        aup = sb("aup", [P, RING, NX])
        adown = sb("adown", [P, RING, NX])
        att = sb("att", [P, 2, 512])
        ys = sb("ys", [P, HEADS, DO])
        clip = sb("clip", [P, HEADS])
        clipl = sb("clipl", [P, HEADS])
        clipr = sb("clipr", [P, HEADS])
        ya = sb("ya", [P, C])
        yb = sb("yb", [P, C])
        yy = sb("yy", [P, RES, C])
        sc = sb("sc", [P, RES, EXPERTS])
        top = sb("top", [P, RES, 8])
        topi = sb("topi", [P, RES, 8], u32)
        topf = sb("topf", [P, RES, 8])
        gd = sb("gd", [P, RES])
        ge = sb("ge", [P, RES])
        g1 = sb("g1", [P, RES])
        g2 = sb("g2", [P, RES])
        gden = sb("gden", [P, RES])
        oh1 = sb("oh1", [P, RES, EXPERTS])
        oh2 = sb("oh2", [P, RES, EXPERTS])
        prob = sb("prob", [P, RES, EXPERTS])
        sh = sb("sh", [P, 2, NTOK])
        hid = sb("hid", [P, 2, HALVES, NTOK])
        acc = sb("acc", [P, RES, C])
        wm = acc[:, 0:6, :].rearrange("p a c -> p (a c)")
        cell = sb("cell", [P, 1])
        pcell = sb("pcell", [P, 1])

        ps = [pb(f"ps{n}") for n in range(8)]
        ps_t, ps_k, ps_y, ps_e, ps_f = ps[0:2], ps[2:4], ps[2], ps[3], [ps[4:6], ps[6:8]]

        s_const, s_mod, s_modst, s_modld = sem("consts_loaded"), sem("mod_done"), sem("mod_stored"), sem("mod_loaded")
        s_silu, s_modps = sem("silu_done"), sem("mod_product")
        s_setup = sem("ones_set")
        s_xc, s_var, s_std, s_h = sem("x_copied"), sem("variance"), sem("deviation"), sem("h_ready")
        s_hst, s_hld, s_hj = sem("h_stored"), sem("h_loaded"), sem("hj_ready")
        s_tp, s_tc = sem("transposed"), sem("transposed_copied")
        s_wps, s_wv, s_tanh, s_par = sem("wave_product"), sem("wave_biased"), sem("tanh_done"), sem("params_ready")
        s_kps, s_kn, s_kst = sem("k_product"), sem("k_ready"), [sem(f"k_stored{n}") for n in range(RES)]
        s_vq, s_kdf, s_w = sem("bin_v_ready"), sem("bin_steps_ready"), sem("tap_counts_read")
        s_ksl = [sem(f"ks_loaded{n}") for n in range(2)]
        s_v, s_cl, s_d, s_up, s_down = sem("v_ready"), sem("v_clamped"), sem("fractions_ready"), sem("up_ready"), sem("down_ready")
        s_aup, s_adown = sem("up_weighted"), sem("down_weighted")
        s_at, s_atc, s_y = sem("a_transposed"), sem("a_copied"), sem("y_product")
        s_yu, s_yy = sem("y_read"), sem("y_ready")
        s_op, s_gp, s_gc, s_gd, s_ge = sem("out_product"), sem("gate_product"), sem("gate_used"), sem("gap_ready"), sem("gap_exp")
        s_f, s_si, s_hid, s_e, s_ac = sem("ff_product"), sem("silu_ready"), sem("hidden_ready"), sem("expert_product"), sem("expert_added")
        s_o, s_out, s_ch = sem("out_ready"), sem("out_stored"), sem("dve_step")
        s_end, s_fin = sem("pass_done"), sem("experts_gated")
        s_m1, s_xr = sem("first_modulation_loaded"), sem("x_in_output")
        AHEAD = 3
        LAST = TILES + 5

        consts = [(rel[:], c_rel), (binpos[:], c_bin), (tokpos[:], c_tok), (ident[:], c_ident), (iota[:], c_iota),
                  (kw[:], kern_wT), (ww[:], wave_wT), (ow[:], out_wT), (gw[:], gateT),
                  (ct[:], cT), (wm, wmod), (w12[:], w12T), (w3[:], w3T.rearrange("k p c -> p k c"))]
        for dst, src, n in ((kbias, kern_b, KALL), (wbias, wave_b, 2 * HEADS)):
            consts.append((dst[:], bass.AP(src.tensor, src.offset, [[0, P], [1, n]])))
        NCONST = 16 * (len(consts) + PAIRS)

        block = ctx.enter_context(nc.Block())

        @block.sync
        def _(sp):
            for dst, src in consts:
                sp.dma_start(dst, src).then_inc(s_const, 16)
            for i in range(PAIRS):
                sp.dma_start(xs[:, i, :], xflat[:, i, :]).then_inc(s_const, 16)
            sp.wait_ge(s_mod, 2)
            sp.dma_start(modscr[:, :], mod[:, :]).then_inc(s_modst, 16)
            sp.wait_ge(s_modst, 16)
            def snap(v):
                return v if isinstance(v, int) else sp.snap(v)

            def pinned(ap):
                return bass.AP(ap.tensor, snap(ap.offset), [list(e) for e in ap.ap])

            def first_modulation(i):
                return [pinned(bass.AP(a.tensor, a.offset, [[0, HP], [1, 2 * C]])) for a in (modscr[bass.ds(2 * i + b, 1), :] for b in range(2))]

            def load_first(src):
                for b in range(2):
                    sp.dma_start(mb1[HP * b:HP * b + HP, :, :].rearrange("p a c -> p (a c)"), src[b]).then_inc(s_m1, 16)

            load_first(first_modulation(0))

            def pair(i, more):
                row = [modscr[bass.ds(2 * i + b, 1), :] for b in range(2)]
                row = [pinned(bass.AP(a.tensor, a.offset, [[0, HP], [1, 6 * C]])) for a in row]
                after = first_modulation(i + 1) if more else None
                hall = hscr[bass.ds(i, 1), :]
                hst = pinned(hall.rearrange("o (p n) -> (o p) n", p=P))
                hin = pinned(hall.rearrange("o (q j c) -> (o j) q c", q=2 * NJ, j=P))
                edges = [(b, e, pinned(bass.AP(hall.tensor, hall.offset + (b * L + tok) * C, [[0, HP], [1, C]])))
                         for b in range(2) for e, tok in ((0, 0), (1, L - 1))]
                n_h, n_hst, n_end = snap(i + 1), snap(16 * i + 16), snap(2 * i + 2)
                sp.wait_ge(s_h, n_h)
                sp.dma_start(hst, yy[:, :, :].rearrange("p r c -> p (r c)")).then_inc(s_hst, 16)
                sp.wait_ge(s_hst, n_hst)
                sp.dma_start(hjr[:, :, :], hin).then_inc(s_hld, 16)
                for b, e, src in edges:
                    sp.dma_start(hedge[HP * b:HP * b + HP, e, :], src).then_inc(s_hld, 16)
                sp.wait_ge(s_end, n_end)
                for b in range(2):
                    sp.dma_start(mb[HP * b:HP * b + HP, :, :].rearrange("p a c -> p (a c)"), row[b]).then_inc(s_modld, 16)
                if more:
                    load_first(after)
                n_kst = snap(16 * i + 16)

                def bins_out(r):
                    dst = pinned(kscr[bass.ds(i, 1), r, :].rearrange("o (p n) -> (o p) n", p=P))
                    n_kn = snap(2 * (RES * i + r + 1))
                    sp.wait_ge(s_kn, n_kn)
                    sp.dma_start(dst, kn[:, r, :, :].rearrange("p h k -> p (h k)")).then_inc(s_kst[r], 16)

                def bins_in(r):
                    kr = kscr[bass.ds(i, 1), r, :]
                    src = [pinned(bass.AP(kr.tensor, kr.offset + b * HP * KALL + BINS // 2 + 1, [[KALL - 1, HP], [1, KALL]])) for b in range(2)]
                    if r == 0:
                        sp.wait_ge(s_kst[0], n_kst)
                    if r == 1:
                        for stored in s_kst[1:]:
                            sp.wait_ge(stored, n_kst)
                    if r >= 2:
                        sp.wait_ge(s_adown, snap(TILES * i + HEADS * (r - 1)))
                    for b in range(2):
                        sp.dma_start(ks[HP * b:HP * b + HP, r % 2, :], src[b]).then_inc(s_ksl[r % 2], 16)

                for r in range(RES):
                    bins_out(r)
                    if r == 2:
                        bins_in(0)
                for r in range(1, RES):
                    bins_in(r)
                if not (isinstance(i, int) and i == 0):
                    store(i - 1)

            def store(f):
                dst = pinned(oflat[bass.ds(f, 1), :, :].rearrange("o p n -> (o p) n"))
                sp.wait_ge(s_o, snap(f + 1))
                sp.dma_start(dst, xo[:, :, :].rearrange("p r c -> p (r c)")).then_inc(s_out, 16)

            pair(0, True)
            with sp.Fori(1, PAIRS - 1) as i:
                pair(i, True)
            pair(PAIRS - 1, False)
            store(PAIRS - 1)
            sp.wait_ge(s_out, 16 * PAIRS)

        @block.gpsimd
        def _(pool):
            c_one = ident[:, 0:1]
            pool.wait_ge(s_const, NCONST)
            for q in range(2 * NJ):
                pool.memset(rows(hj[:, q, D:D + 1], [[DO, HEADS]]), 1.0).then_inc(s_setup, 1)
            pool.wait_ge(s_setup, 2 * NJ)
            def pair(i):
                pool.wait_ge(s_end, 2 * i + 2)
                pool.wait_ge(s_hld, 80 * (i + 1))
                pool.tensor_tensor(pcell[:, :], c_one, c_one, ALU.mult)
                for q in range(2 * NJ):
                    pool.tensor_copy(hj[:, q, :].rearrange("p (h d) -> p h d", d=DO)[:, :, 0:D],
                                     hjr[:, q, :].rearrange("p (h d) -> p h d", d=D)).then_inc(s_hj, 1)
                pool.wait_ge(s_par, i + 1)
                for r in range(RES):
                    if r >= 2:
                        pool.wait_ge(s_w, RES * i + r - 1)
                    if r >= 1:
                        pool.wait_ge(s_vq, 2 * (RES * i + r))
                    pool.tensor_tensor(vq[:, :, :], rows(binpos[:, :], [[0, HEADS], [1, BINS - 1]]),
                                       rows(pscale[:, r, :], [[1, HEADS], [0, BINS - 1]]), ALU.mult).then_inc(s_vq, 1)
                    pool.wait_ge(s_vq, 2 * (RES * i + r) + 1)
                    pool.tensor_tensor(vq2[:, r % 2, :, :], vq[:, :, :],
                                       rows(pbias[:, r, :], [[1, HEADS], [0, BINS - 1]]), ALU.add).then_inc(s_vq, 1)
                    pool.wait_ge(s_kn, 2 * (RES * i + r + 1))
                    pool.tensor_tensor(kdiff[:, r % 2, :, :], kn[:, r, :, 3:2 + BINS],
                                       kn[:, r, :, 2:1 + BINS], ALU.subtract).then_inc(s_kdf, 1)

            pair(0)
            with pool.Fori(1, PAIRS) as i:
                pair(i)

        @block.scalar
        def _(act):
            act.wait_ge(s_const, NCONST)
            act.activation(cs[:, :], ct[:, :], ACT.Silu).then_inc(s_silu, 1)
            act.wait_ge(s_modps, 2)
            for n in range(2):
                act.activation(mod[:, n * 384:n * 384 + 384], ps[n][0:B, 0:384], ACT.Copy).then_inc(s_silu, 1)
            def gated(f, t):
                u = (t - 2) // 2
                if t % 2 == 0 and 0 <= u < 2 * EXPERTS * HALVES:
                    act.wait_ge(s_f, 64 * f + 2 * u + 1)
                    if u >= 2:
                        act.wait_ge(s_hid, 32 * f + u - 1)
                    act.activation(sh[:, u % 2, :], ps_f[u % 2][0][:, :], ACT.Silu).then_inc(s_si, 1)

            def fetched(i):
                act.activation(xc[:, :, :].rearrange("p r c -> p (r c)"), xs[:, bass.ds(i, 1), :].rearrange("p o n -> p (o n)"),
                               ACT.Copy).then_inc(s_xc, 1)

            fetched(0)
            act.wait_ge(s_var, 1)
            act.activation(std[:, :], var[:, :], ACT.Sqrt).then_inc(s_std, 1)

            def pair(i, experts, more):
                for n in range(2):
                    act.wait_ge(s_tp, 6 * i + n + 1)
                    act.activation(ht[:, 4 * n:4 * n + 4, :].rearrange("p r t -> p (r t)"), ps_t[n][:, :], ACT.Copy).then_inc(s_tc, 1)
                act.wait_ge(s_end, 2 * i + 2)
                act.wait_ge(s_wv, i + 1)
                act.activation(freq[:, :, :], rows(wv[:, 0, 0:1], [[2, TILES]]), ACT.Tanh, scale=0.5).then_inc(s_tanh, 1)
                act.activation(shift[:, :, :], rows(wv[:, 0, 1:2], [[2, TILES]]), ACT.Tanh).then_inc(s_tanh, 1)
                act.wait_ge(s_par, i + 1)

                def scaled(t):
                    r, h = t // HEADS, t % HEADS
                    if t >= 2:
                        act.wait_ge(s_cl, 2 * (TILES * i + t - 1))
                    act.activation(vt[:, t % 2, :], rel[:, :], ACT.Identity, bias=pbias[:, r, h:h + 1],
                                   scale=pscale[:, r, h:h + 1]).then_inc(s_v, 1)

                def copied(t):
                    act.wait_ge(s_at, TILES * i + t + 1)
                    if t >= 2:
                        act.wait_ge(s_y, TILES * i + t - 1)
                    act.activation(att[:, t % 2, :], ps_t[t % 2][:, :], ACT.Copy).then_inc(s_atc, 1)

                scaled(0)
                scaled(1)
                if more:
                    fetched(i + 1)
                for t in range(TILES):
                    r, h = t // HEADS, t % HEADS
                    act.wait_ge(s_d, TILES * i + t + 1)
                    if t >= 2:
                        act.wait_ge(s_aup, TILES * i + t - 1)
                    act.activation(up[:, t % 2, :], frac[:, t % 2, 0, 0:NX], ACT.Relu, bias=ufloor[:, r, h:h + 1]).then_inc(s_up, 1)
                    if t >= 2:
                        act.wait_ge(s_adown, TILES * i + t - 1)
                    act.activation(down[:, t % 2, :], frac[:, t % 2, 1, 1:NX + 1], ACT.Relu, bias=dcap[:, r, h:h + 1], scale=-1.0).then_inc(s_down, 1)
                    if t + 2 < TILES:
                        scaled(t + 2)
                    if t >= 2:
                        copied(t - 2)
                    if experts:
                        gated(i - 1, t)
                copied(TILES - 2)
                copied(TILES - 1)
                if experts:
                    for t in range(TILES, LAST):
                        gated(i - 1, t)
                for n in range(2):
                    act.wait_ge(s_tp, 6 * i + 2 + n + 1)
                    act.activation(ht[:, 4 * n:4 * n + 4, :].rearrange("p r t -> p (r t)"), ps_t[n][:, :], ACT.Copy).then_inc(s_tc, 1)
                if more:
                    act.wait_ge(s_var, 2 * i + 2)
                    act.activation(std[:, :], var[:, :], ACT.Sqrt).then_inc(s_std, 1)
                if experts:
                    act.wait_ge(s_out, 16 * i)
                act.activation(xo[:, :, :].rearrange("p r c -> p (r c)"), xs[:, bass.ds(i, 1), :].rearrange("p o n -> p (o n)"),
                               ACT.Copy).then_inc(s_xr, 1)
                act.wait_ge(s_var, 2 * i + (3 if more else 2))
                act.activation(std[:, :], var[:, :], ACT.Sqrt).then_inc(s_std, 1)
                for n in range(2):
                    act.wait_ge(s_tp, 6 * i + 4 + n + 1)
                    act.activation(h2t[:, 4 * n:4 * n + 4, :].rearrange("p r t -> p (r t)"), ps_t[n][:, :], ACT.Copy).then_inc(s_tc, 1)
                act.wait_ge(s_gd, i + 1)
                act.activation(ge[:, :], gd[:, :], ACT.Exp).then_inc(s_ge, 1)

            pair(0, False, True)
            with act.Fori(1, PAIRS - 1) as i:
                pair(i, True, True)
            pair(PAIRS - 1, True, False)
            for t in range(LAST):
                gated(PAIRS - 1, t)

        @block.tensor
        def _(pe):
            pe.wait_ge(s_silu, 1)
            for n in range(2):
                nc.tensor.matmul(ps[n][0:B, 0:384], cs[:, :], wm[:, n * 384:n * 384 + 384], start=True, stop=True).then_inc(s_modps, 1)
            pe.wait_ge(s_silu, 3)
            def pair(i, experts):
                def turned(src, n):
                    for r in range(4):
                        last = nc.tensor.transpose(ps_t[n][:, r * P:r * P + P], src[:, 4 * n + r, :], ident[:, :])
                    last.then_inc(s_tp, 1)

                pe.wait_ge(s_h, i + 1)
                if experts:
                    pe.wait_ge(s_gd, i)
                for n in range(2):
                    turned(yy, n)
                pe.wait_ge(s_tc, 6 * i + 2)
                for r in range(RES):
                    last = nc.tensor.matmul(ps_f[1][1][:, r * 16:r * 16 + 16], ht[:, r, :], ww[:, :], start=True, stop=True)
                last.then_inc(s_wps, 1)
                for c in range(2 * RES):
                    cols = slice(KHALF * (c % 2), KHALF * (c % 2) + KHALF)
                    if c >= 2:
                        pe.wait_ge(s_kn, 2 * RES * i + c - 1)
                    nc.tensor.matmul(ps_k[c % 2][:, 0:KHALF], ht[:, c // 2, :], kw[:, cols], start=True, stop=True).then_inc(s_kps, 1)
                pe.wait_ge(s_kn, 2 * RES * (i + 1))
                pe.wait_ge(s_hj, 2 * NJ * (i + 1))

                def weigh(t):
                    r, h = t // HEADS, t % HEADS
                    pe.wait_ge(s_atc, TILES * i + t + 1)
                    if h == 0 and r >= 1:
                        pe.wait_ge(s_yu, RES * i + r)
                    for b in range(2):
                        for j in range(NJ):
                            last = nc.tensor.matmul(ps_y[HP * b:HP * b + HP, h * DO:h * DO + DO],
                                                    att[:, t % 2, j * P + HP * b:j * P + HP * b + HP],
                                                    hj[:, b * NJ + j, h * DO:h * DO + DO], start=(j == 0), stop=(j == NJ - 1))
                    last.then_inc(s_y, 1)

                for t in range(TILES):
                    r = t // HEADS
                    pe.wait_ge(s_aup, TILES * i + t + 1)
                    pe.wait_ge(s_adown, TILES * i + t + 1)
                    if t >= 2:
                        pe.wait_ge(s_atc, TILES * i + t - 1)
                    for j in range(NJ):
                        o = RES - r + j * P
                        dst = ps_t[t % 2][:, j * P:j * P + P]
                        nc.tensor.matmul(dst, aup[:, t % RING, o:o + P], ident[:, :], is_transpose=True, start=True, stop=False)
                        last = nc.tensor.matmul(dst, adown[:, t % RING, o - 1:o - 1 + P], ident[:, :], is_transpose=True, start=False, stop=True)
                    last.then_inc(s_at, 1)
                    if t >= 2:
                        weigh(t - 2)
                    if experts:
                        experts_step(i - 1, t)
                weigh(TILES - 2)
                weigh(TILES - 1)
                if experts:
                    for t in range(TILES, LAST):
                        experts_step(i - 1, t)
                pe.wait_ge(s_yy, RES * (i + 1))
                for n in range(2):
                    turned(yy, n)
                pe.wait_ge(s_tc, 6 * i + 4)
                if experts:
                    pe.wait_ge(s_ac, 64 * i)
                for r in range(RES):
                    last = nc.tensor.matmul(ps_k[r // 4][:, (r % 4) * C:(r % 4) * C + C], ht[:, r, :], ow[:, :], start=True, stop=True)
                last.then_inc(s_op, 1)
                pe.wait_ge(s_gc, i + 1)
                for n in range(2):
                    turned(hn, n)
                pe.wait_ge(s_tc, 6 * i + 6)
                for r in range(RES):
                    last = nc.tensor.matmul(ps_t[0][:, r * 8:r * 8 + 8], h2t[:, r, :], gw[:, :], start=True, stop=True)
                last.then_inc(s_gp, 1)

            def experts_step(f, t):
                u, part, v, g = t // 2, t % 2, (t - 6) // 4, (t - 6) % 4
                if u < 2 * EXPERTS * HALVES:
                    q, e, k = u // 16, u // 2 % EXPERTS, u % 2
                    if u >= 2 and part == 0:
                        pe.wait_ge(s_hid, 32 * f + u - 1)
                    o = e * 2 * FF + part * FF + k * P
                    nc.tensor.matmul(ps_f[u % 2][part][:, :], w12[:, o:o + P],
                                     h2t[:, RPT * q:RPT * q + RPT, :].rearrange("p r t -> p (r t)"), start=True, stop=True).then_inc(s_f, 1)
                if g < 2 and 0 <= v < 2 * EXPERTS:
                    e = v % EXPERTS
                    if g == 0:
                        pe.wait_ge(s_hid, 32 * f + 2 * v + 2)
                        if v >= 1:
                            pe.wait_ge(s_ac, 64 * f + RPT * v)
                    for m in (2 * g, 2 * g + 1):
                        for k in range(HALVES):
                            last = nc.tensor.matmul(ps_e[:, m * C:m * C + C], hid[:, v % 2, k, m * P:m * P + P],
                                                    w3[:, e * HALVES + k, :], start=(k == 0), stop=(k == HALVES - 1))
                    if g == 1:
                        last.then_inc(s_e, 1)

            pair(0, False)
            with pe.Fori(1, PAIRS) as i:
                pair(i, True)
            for t in range(LAST):
                experts_step(PAIRS - 1, t)

        CHAIN = chain_len()

        @block.vector
        def _(dve):
            n = [0]
            base = [0]

            def link(ins):
                n[0] += 1
                ins.then_inc(s_ch, 1)
                dve.wait_ge(s_ch, base[0] + n[0])

            def fence():
                nc.vector.memset(cell[:, :], 0.0)

            dve.wait_ge(s_silu, 3)
            for a in (1, 4):
                link(nc.vector.tensor_scalar(mod[:, a * C:a * C + C], mod[:, a * C:a * C + C], 1.0, None, ALU.add))
            for a in (2, 5):
                g = mod[:, a * C:a * C + C]
                nc.vector.tensor_scalar(msign[:, :], g, 0.0, 2.0, ALU.is_ge, ALU.mult)
                link(nc.vector.scalar_tensor_tensor(mabs[:, :], g, -1.0, g, ALU.mult, ALU.max))
                link(nc.vector.tensor_scalar(mabs[:, :], mabs[:, :], 0.25, None, ALU.max))
                link(nc.vector.tensor_scalar(msign[:, :], msign[:, :], -1.0, None, ALU.add))
                nc.vector.tensor_tensor(g, msign[:, :], mabs[:, :], ALU.mult).then_inc(s_mod, 1)
                dve.wait_ge(s_mod, 1 if a == 2 else 2)
            setup = n[0]
            nc.vector.memset(cell[:, :], 0.0).then_inc(s_end, 2)

            def experts_step(f, t):
                u, v = (t - 3) // 2, (t - 8) // 4
                if t % 2 == 1 and 0 <= u < 2 * EXPERTS * HALVES:
                    dve.wait_ge(s_si, 32 * f + u + 1)
                    dve.wait_ge(s_f, 64 * f + 2 * u + 2)
                    if u >= 4:
                        dve.wait_ge(s_e, 16 * f + u // 2 - 1)
                    nc.vector.tensor_tensor(hid[:, u // 2 % 2, u % 2, :], sh[:, u % 2, :], ps_f[u % 2][1][:, :], ALU.mult).then_inc(s_hid, 1)
                if t % 4 == 0 and 0 <= v < 2 * EXPERTS:
                    q, e = v // EXPERTS, v % EXPERTS
                    dve.wait_ge(s_e, 16 * f + v + 1)
                    if e:
                        dve.wait_ge(s_ac, 64 * f + RPT * v)
                    for m in range(RPT):
                        r = q * RPT + m
                        o = ps_e[:, m * C:m * C + C]
                        if e == 0:
                            nc.vector.tensor_scalar(acc[:, r, :], o, prob[:, r, 0:1], None, ALU.mult).then_inc(s_ac, 1)
                        else:
                            nc.vector.scalar_tensor_tensor(acc[:, r, :], o, prob[:, r, e:e + 1], acc[:, r, :], ALU.mult, ALU.add).then_inc(s_ac, 1)

            def finished(f):
                dve.wait_ge(s_ac, 64 * f + 64)
                nc.vector.tensor_tensor(acc[:, :, :], acc[:, :, :], rows(gb[:, :], [[0, RES], [1, C]]), ALU.mult).then_inc(s_fin, 1)
                dve.wait_ge(s_fin, f + 1)
                nc.vector.tensor_tensor(xo[:, :, :], xo[:, :, :], acc[:, :, :], ALU.add).then_inc(s_o, 1)

            def deviations(which, k, src):
                variances(which, src)
                inverted(which, k)

            def variances(which, src):
                for r in range(RES):
                    ins = nc.vector.bn_stats(stats[:, r, :], src[:, r, :])
                link(ins)
                fence()
                for r in range(RES):
                    ins = nc.vector.bn_aggr(mv[:, which, r, :], stats[:, r, :])
                link(ins)
                nc.vector.tensor_scalar(var[:, :], rows(mv[:, which, 0, 1:2], [[2, RES]]), EPS, None, ALU.add).then_inc(s_var, 1)

            def inverted(which, k):
                dve.wait_ge(s_std, k)
                y = rstd[:, which, :]
                link(nc.vector.reciprocal(y, std[:, :]))
                link(nc.vector.tensor_tensor(rtmp[:, :], y, y, ALU.mult))
                link(nc.vector.tensor_tensor(rtmp[:, :], rtmp[:, :], var[:, :], ALU.mult))
                link(nc.vector.tensor_scalar(rtmp[:, :], rtmp[:, :], -0.5, 1.5, ALU.mult, ALU.add))
                link(nc.vector.tensor_tensor(y, y, rtmp[:, :], ALU.mult))

            def normed(which, src, dst, scale, bias, done):
                for r in range(RES):
                    ins = nc.vector.tensor_scalar(dst[:, r, :], src[:, r, :], mv[:, which, r, 0:1], rstd[:, which, r:r + 1], ALU.subtract, ALU.mult)
                link(ins)
                link(nc.vector.tensor_tensor(dst[:, :, :], dst[:, :, :], rows(scale, [[0, RES], [1, C]]), ALU.mult))
                nc.vector.tensor_tensor(dst[:, :, :], dst[:, :, :], rows(bias, [[0, RES], [1, C]]), ALU.add).then_inc(done, 1)

            dve.wait_ge(s_xc, 1)
            deviations(0, 1, xc)
            dve.wait_ge(s_m1, 32)
            normed(0, xc, yy, mb1[:, 1, :], mb1[:, 0, :], s_h)
            setup = n[0]

            def pair(i, experts, more):
                n[0] = 0
                base[0] = CHAIN * i + setup
                T0 = TILES * i

                dve.wait_ge(s_wps, i + 1)
                nc.vector.tensor_tensor(wv[:, :, :], ps_f[1][1][:, 0:RES * 16].rearrange("p (r w) -> p r w", w=16),
                                        rows(wbias[:, :], [[0, RES], [1, 2 * HEADS]]), ALU.add).then_inc(s_wv, 1)
                dve.wait_ge(s_tanh, 2 * (i + 1))
                half = (MAX_FREQ - MIN_FREQ) / 2
                link(nc.vector.tensor_scalar(freq[:, :, :], freq[:, :, :], half, MIN_FREQ + half, ALU.mult, ALU.add))
                link(nc.vector.reciprocal(inv[:, :, :], freq[:, :, :]))
                nc.vector.tensor_tensor(left[:, :, :], freq[:, :, :], shift[:, :, :], ALU.mult)
                link(nc.vector.tensor_scalar(pscale[:, :, :], inv[:, :, :], float(UNIT), None, ALU.mult))
                nc.vector.tensor_scalar(pbias[:, :, :], shift[:, :, :], -float(UNIT), 15.5 * UNIT - 1, ALU.mult, ALU.add)
                nc.vector.tensor_scalar(dcap[:, :, :], pscale[:, :, :], -1.0, None, ALU.add)
                link(nc.vector.tensor_scalar(posf[:, :, :], freq[:, :, :], 1.0 / UNIT, None, ALU.mult))
                nc.vector.tensor_scalar(ufloor[:, :, :], pscale[:, :, :], -float(UNIT - 1), 0.0, ALU.add, ALU.min)
                link(nc.vector.tensor_tensor(left[:, :, :], left[:, :, :], rows(tokpos[:, :], [[1, RES], [0, HEADS]]), ALU.add))
                nc.vector.tensor_scalar(left[:, :, :], left[:, :, :], L / 2.0, None, ALU.is_lt).then_inc(s_par, 1)

                def total(r):
                    dve.wait_ge(s_vq, 2 * (RES * i + r + 1))
                    link(nc.vector.tensor_scalar(tq[:, :, :], vq2[:, r % 2, :, :], -1.0, float(TAPS * UNIT - 1), ALU.max, ALU.min))
                    link(nc.vector.tensor_scalar(tq2[:, :, :], tq[:, :, :], 19, None, ALU.arith_shift_right))
                    dve.wait_ge(s_kdf, RES * i + r + 1)
                    link(nc.vector.scalar_tensor_tensor(tk[:, :, :], tq2[:, :, :], 1.0, kdiff[:, r % 2, :, :], ALU.add, ALU.mult))
                    link(nc.vector.reduce_sum(red[:, :], tk[:, :, :], AX.X))
                    nc.vector.scalar_tensor_tensor(wtot[:, r, :], rows(kn[:, r, 0, 1 + BINS:2 + BINS], [[KROW, HEADS]]), float(TAPS), red[:, :],
                                                   ALU.mult, ALU.subtract).then_inc(s_w, 1)

                def clamped(t):
                    dve.wait_ge(s_v, T0 + t + 1)
                    if t >= 1:
                        dve.wait_ge(s_d, T0 + t)
                    nc.vector.tensor_scalar(xt[:, 0, :], vt[:, t % 2, :], -float(UNIT), float((TAPS - 1) * UNIT), ALU.max, ALU.min).then_inc(s_cl, 1)
                    nc.vector.tensor_scalar(xt[:, 1, :], vt[:, t % 2, :], -1.0, float(TAPS * UNIT - 1), ALU.max, ALU.min).then_inc(s_cl, 1)

                def fractions(t):
                    dve.wait_ge(s_cl, 2 * (T0 + t + 1))
                    if t >= 2:
                        dve.wait_ge(s_up, T0 + t - 1)
                        dve.wait_ge(s_down, T0 + t - 1)
                    nc.vector.tensor_scalar(frac[:, t % 2, :, :], xt[:, :, :], UNIT - 1, None, ALU.bitwise_and).then_inc(s_d, 1)

                def weighted(t, part, out_, ready, done):
                    r, h = t // HEADS, t % HEADS
                    dve.wait_ge(ready, T0 + t + 1)
                    if t >= RING:
                        dve.wait_ge(s_at, T0 + t - RING + 1)
                    ins = nc.vector.tensor_tensor(out_[:, t % RING, :].rearrange("p (g k) -> p g k", k=8), part[:, t % 2, :].rearrange("p (g k) -> p g k", k=8),
                                                  rows(ks[:, r % 2, h * KROW:h * KROW + 1], [[1, NG], [0, 8]]), ALU.mult)
                    ins.then_inc(done, 1)

                def combined(r):
                    dve.wait_ge(s_y, T0 + HEADS * (r + 1))
                    if r == 0:
                        dve.wait_ge(s_hld, 80 * (i + 1))
                    dve.wait_ge(s_w, RES * i + r + 1)
                    nc.vector.tensor_tensor(ys[:, :, :], ps_y[:, 0:HEADS * DO].rearrange("p (h d) -> p h d", d=DO),
                                            rows(posf[:, r, :], [[1, HEADS], [0, DO]]), ALU.mult).then_inc(s_yu, 1)
                    dve.wait_ge(s_yu, RES * i + r + 1)
                    link(nc.vector.tensor_tensor(clip[:, :], wtot[:, r, :], rows(ys[:, 0, D:D + 1], [[DO, HEADS]]), ALU.subtract))
                    link(nc.vector.tensor_tensor(clipl[:, :], clip[:, :], left[:, r, :], ALU.mult))
                    link(nc.vector.tensor_tensor(clipr[:, :], clip[:, :], clipl[:, :], ALU.subtract))
                    v = [a[:, :].rearrange("p (h d) -> p h d", d=D) for a in (ya, yb)]
                    nc.vector.tensor_tensor(v[0], hedge[:, 0, :].rearrange("p (h d) -> p h d", d=D), rows(clipl[:, :], [[1, HEADS], [0, D]]), ALU.mult)
                    link(nc.vector.tensor_tensor(v[1], hedge[:, 1, :].rearrange("p (h d) -> p h d", d=D), rows(clipr[:, :], [[1, HEADS], [0, D]]), ALU.mult))
                    link(nc.vector.tensor_tensor(ya[:, :], ya[:, :], yb[:, :], ALU.add))
                    nc.vector.tensor_tensor(yy[:, r, :].rearrange("p (h d) -> p h d", d=D), v[0], ys[:, :, 0:D], ALU.add).then_inc(s_yy, 1)

                for c in range(2 * RES):
                    dve.wait_ge(s_kps, 2 * RES * i + c + 1)
                    nc.vector.tensor_tensor(rows(kn[:, c // 2, HEADS // 2 * (c % 2), 0:1], [[1, KHALF]]), ps_k[c % 2][:, 0:KHALF],
                                            kbias[:, KHALF * (c % 2):KHALF * (c % 2) + KHALF], ALU.add).then_inc(s_kn, 1)
                    if c in (7, 11, 15):
                        total((c - 7) // 4)
                clamped(0)
                fractions(0)
                for t in range(TILES):
                    r, h = t // HEADS, t % HEADS
                    if t + 1 < TILES:
                        clamped(t + 1)
                    if h == 0:
                        dve.wait_ge(s_ksl[r % 2], 32 * (RES // 2 * i + r // 2 + 1))
                    weighted(t, up, aup, s_up, s_aup)
                    if t + 1 < TILES:
                        fractions(t + 1)
                    weighted(t, down, adown, s_down, s_adown)
                    if h == 3 and r >= 1:
                        combined(r - 1)
                    if h == 4 and r + AHEAD < RES:
                        total(r + AHEAD)
                    if experts:
                        experts_step(i - 1, t)
                if experts:
                    experts_step(i - 1, TILES)
                if more:
                    dve.wait_ge(s_xc, i + 2)
                    variances(0, xc)
                if experts:
                    experts_step(i - 1, TILES + 1)
                combined(RES - 1)
                if experts:
                    for t in range(TILES + 2, LAST):
                        experts_step(i - 1, t)
                    finished(i - 1)
                if more:
                    inverted(0, 2 * i + 2)

                dve.wait_ge(s_op, i + 1)
                dve.wait_ge(s_modld, 32 * (i + 1))
                for m in range(2):
                    o = ps_k[m][:, :].rearrange("p (r c) -> p r c", c=C)
                    link(nc.vector.tensor_tensor(hn[:, 4 * m:4 * m + 4, :], o, rows(mb[:, 2, :], [[0, 4], [1, C]]), ALU.mult))
                dve.wait_ge(s_xr, i + 1)
                link(nc.vector.tensor_tensor(xo[:, :, :], xo[:, :, :], hn[:, :, :], ALU.add))
                deviations(1, 2 * i + (3 if more else 2), xo)
                normed(1, xo, hn, mb[:, 4, :], mb[:, 3, :], s_gc)
                if more:
                    dve.wait_ge(s_tp, 6 * i + 4)
                    dve.wait_ge(s_m1, 32 * (i + 2))
                    normed(0, xc, yy, mb1[:, 1, :], mb1[:, 0, :], s_h)

                dve.wait_ge(s_gp, i + 1)
                link(nc.vector.tensor_copy(sc[:, :, :], ps_t[0][:, 0:RES * 8].rearrange("p (r e) -> p r e", e=8)))
                fence()
                for r in range(RES):
                    ins = nc.vector.max(top[:, r, :], sc[:, r, :])
                link(ins)
                fence()
                for r in range(RES):
                    ins = nc.vector.max_index(topi[:, r, :], top[:, r, :], sc[:, r, :])
                link(ins)
                nc.vector.tensor_tensor(gd[:, :], rows(top[:, 0, 1:2], [[8, RES]]), rows(top[:, 0, 0:1], [[8, RES]]), ALU.subtract).then_inc(s_gd, 1)
                link(nc.vector.tensor_copy(topf[:, :, :], topi[:, :, :]))
                it = rows(iota[:, :], [[0, RES], [1, EXPERTS]])
                nc.vector.tensor_tensor(oh1[:, :, :], it, rows(topf[:, 0, 0:1], [[8, RES], [0, EXPERTS]]), ALU.is_equal)
                nc.vector.tensor_tensor(oh2[:, :, :], it, rows(topf[:, 0, 1:2], [[8, RES], [0, EXPERTS]]), ALU.is_equal)
                dve.wait_ge(s_ge, i + 1)
                link(nc.vector.tensor_scalar(gden[:, :], ge[:, :], 1.0, None, ALU.add))
                link(nc.vector.reciprocal(g1[:, :], gden[:, :]))
                link(nc.vector.tensor_tensor(g2[:, :], g1[:, :], ge[:, :], ALU.mult))
                nc.vector.tensor_tensor(oh1[:, :, :], oh1[:, :, :], rows(g1[:, :], [[1, RES], [0, EXPERTS]]), ALU.mult)
                link(nc.vector.tensor_tensor(oh2[:, :, :], oh2[:, :, :], rows(g2[:, :], [[1, RES], [0, EXPERTS]]), ALU.mult))
                link(nc.vector.tensor_tensor(prob[:, :, :], oh1[:, :, :], oh2[:, :, :], ALU.add))

                nc.vector.tensor_copy(gb[:, :], mb[:, 5, :]).then_inc(s_end, 2)
                assert n[0] == CHAIN or not more, n[0]

            pair(0, False, True)
            with dve.Fori(1, PAIRS - 1) as i:
                pair(i, True, True)
            pair(PAIRS - 1, True, False)
            for t in range(LAST):
                experts_step(PAIRS - 1, t)
            finished(PAIRS - 1)


def chain_len():
    norm = 2 + 5 + 2
    params = 5
    bins = RES * 4
    tiles = 0
    combine = RES * 5
    tail = 3
    gate = 3 + 1 + 3 + 2
    return 2 * norm + params + bins + tiles + combine + tail + gate


def kernel(**inputs):
    import numpy as np
    import concourse.bacc as bacc
    from concourse.bass_utils import run_bass_kernel_spmd as run

    f = np.float32
    g = {k: np.asarray(v) for k, v in inputs.items()}
    p = np.arange(P)
    tok = 8 * (p % HP)
    cols = (BINS * np.arange(HEADS)[:, None] + np.clip(np.arange(KROW) - 2, 0, BINS - 1)[None, :]).reshape(-1)
    arrays = {
        "x": g["L0_attn_x"],
        "wave_wT": g["L0_attn_wave_w"].T, "wave_b": g["L0_attn_wave_b"],
        "kern_wT": g["L0_attn_kernel_w"].T[:, cols], "kern_b": g["L0_attn_kernel_b"][cols],
        "out_wT": g["L0_attn_out_w"].T,
        "w12T": g["L0_ffn_w12"].reshape(EXPERTS * 2 * FF, C).T,
        "w3T": g["L0_ffn_w3"].transpose(0, 2, 1).reshape(EXPERTS * HALVES, P, C),
        "gateT": g["L0_ffn_gate_w"].T, "cT": g["L0_c"].T, "wmod": g["L0_wmod"],
        "c_rel": (np.arange(NV)[None, :] - 8 - tok[:, None]).astype(f),
        "c_bin": np.broadcast_to(8 * np.arange(1, BINS) - L // 2, (P, BINS - 1)).astype(f),
        "c_tok": (tok[:, None] + np.arange(RES)[None, :]).astype(f),
        "c_ident": np.eye(P, dtype=f),
        "c_iota": np.broadcast_to(np.arange(EXPERTS), (P, EXPERTS)).astype(f),
    }
    nc = bacc.Bacc("TRN2", target_bir_lowering=False, num_devices=1)
    data, args = {}, []
    for name, a in arrays.items():
        a = np.ascontiguousarray(a)
        data[f"in_{name}"] = a
        args.append(nc.dram_tensor(f"in_{name}", a.shape, mybir.dt.from_np(a.dtype), kind="ExternalInput").ap())
    args.append(nc.dram_tensor("out_0", (B, L, C), mybir.dt.float32, kind="ExternalOutput").ap())
    build(nc, *args)
    r = run(nc, [data], core_ids=[0])
    return r.results[0]["out_0"]
```
